# Optimizing a Trainium2 kernel written in Bass

```python
import numpy as np
import jax
import jax.numpy as jnp

def _softmax(x, axis=-1):
    return jax.nn.softmax(x, axis=axis)

def _gelu(x):
    return jax.nn.gelu(x, approximate=True)

def _silu(x):
    return jax.nn.silu(x)

def _sigmoid(x):
    return jax.nn.sigmoid(x)

def _layernorm(x, axis=-1, eps=1e-05):
    m = jnp.mean(x, axis=axis, keepdims=True)
    v = jnp.var(x, axis=axis, keepdims=True)
    return (x - m) / jnp.sqrt(v + eps)

def _scatter_add(tgt, idx, src, axis=0):
    return tgt.at[idx].add(src)

def _segment_sum(src, seg, n):
    return jax.ops.segment_sum(src, seg, n)
kernel_name = 'mk_prb_d4_jaxref_r8_6a415f'

def setup_inputs(seed: int=0):
    np.random.seed(seed)
    _w = jnp.asarray

    def _L0_attn_setup():
        import jax, jax.numpy as jnp
        import numpy as np
        EMBED = 128
        HEADS = 16
        key = jax.random.key(seed)
        ks = jax.random.split(key, 6)
        N, S = (1, 512)
        half = EMBED // 2
        x = jax.random.normal(ks[0], (N, S, EMBED), dtype=jnp.float32)
        Wq = jax.random.normal(ks[1], (half, half), dtype=jnp.float32) * 0.02
        Wk = jax.random.normal(ks[2], (half, half), dtype=jnp.float32) * 0.02
        Wv = jax.random.normal(ks[3], (half, half), dtype=jnp.float32) * 0.02
        Wo = jax.random.normal(ks[4], (EMBED, half), dtype=jnp.float32) * 0.02
        bo = jnp.zeros((EMBED,), dtype=jnp.float32)
        return {'x': x, 'Wq': Wq, 'Wk': Wk, 'Wv': Wv, 'Wo': Wo, 'bo': bo}
    _L0_attn_in = _L0_attn_setup()

    def _L0_ffn_setup():
        import jax, jax.numpy as jnp
        import numpy as np
        D = 128
        H = 16
        HD = D // H
        L = 64
        E = 8
        B, T = (4, 256)
        EPS = 1e-06

        def _glorot(k, shape):
            fan_in, fan_out = (shape[-2], shape[-1])
            lim = np.sqrt(6.0 / (fan_in + fan_out)).astype(np.float32)
            return jax.random.uniform(k, shape, jnp.float32, -lim, lim)

        def _rmsnorm(x, gamma):
            return gamma * x * jax.lax.rsqrt(jnp.mean(x * x, axis=-1, keepdims=True) + EPS)
        key = jax.random.key(seed)
        ks = jax.random.split(key, 8)
        return {'x': jax.random.normal(ks[0], (B, T, D), jnp.float32), 'gamma1': jnp.ones((D,), jnp.float32), 'Wq': _glorot(ks[1], (D, D)), 'bq': jnp.zeros((D,), jnp.float32), 'Wdown': _glorot(ks[2], (D, L)), 'bdown': jnp.zeros((L,), jnp.float32), 'Wup': _glorot(ks[3], (L, 2 * D)), 'bup': jnp.zeros((2 * D,), jnp.float32), 'Wo': _glorot(ks[4], (D, D)), 'bo': jnp.zeros((D,), jnp.float32), 'gamma2': jnp.ones((D,), jnp.float32), 'Wg': _glorot(ks[5], (D, E)), 'bg': jnp.zeros((E,), jnp.float32), 'We': _glorot(ks[6], (E, D, D))}
    _L0_ffn_in = _L0_ffn_setup()

    def _L1_attn_setup():
        import jax, jax.numpy as jnp
        import numpy as np
        D = 128
        H = 16
        HD = D // H
        B = 2
        T = 256

        def _apply_rotary(x, rope):
            x1, x2 = (x[..., ::2], x[..., 1::2])
            sin, cos = (rope[..., ::2], rope[..., 1::2])
            return jnp.concatenate([x1 * cos - x2 * sin, x1 * sin + x2 * cos], axis=-1)
        key = jax.random.key(seed)
        k0, k1, k2 = jax.random.split(key, 3)
        s = 1.0 / np.sqrt(D)
        return {'x': jax.random.normal(k0, (B, T, D), dtype=jnp.float32), 'qkv_w': jax.random.normal(k1, (D, 3 * D), dtype=jnp.float32) * s, 'qkv_b': jnp.zeros((3 * D,), dtype=jnp.float32), 'out_w': jax.random.normal(k2, (D, D), dtype=jnp.float32) * s, 'out_b': jnp.zeros((D,), dtype=jnp.float32)}
    _L1_attn_in = _L1_attn_setup()

    def _L1_ffn_setup():
        import jax, jax.numpy as jnp
        import numpy as np
        DIM = 128
        HIDDEN = 384
        SCALE = 1.0 / 127.0

        def _dequant(w_int, dtype):
            return w_int.astype(dtype) * jnp.asarray(SCALE, dtype)
        key = jax.random.key(seed)
        k_x, k_g, k_u, k_d = jax.random.split(key, 4)
        x = jax.random.normal(k_x, (4, 256, DIM), dtype=jnp.float32)
        w_gate = jax.random.randint(k_g, (HIDDEN, DIM), -127, 128, dtype=jnp.int32)
        w_up = jax.random.randint(k_u, (HIDDEN, DIM), -127, 128, dtype=jnp.int32)
        w_down = jax.random.randint(k_d, (DIM, HIDDEN), -127, 128, dtype=jnp.int32)
        return {'x': x, 'w_gate': w_gate, 'w_up': w_up, 'w_down': w_down}
    _L1_ffn_in = _L1_ffn_setup()

    def _L2_attn_setup():
        import jax, jax.numpy as jnp
        import numpy as np
        import math
        THETA = 500.0
        SCALE = 1.0
        NUM_HEADS = 16

        def apply_rope(t, theta=THETA, scale=SCALE):
            D = t.shape[-1]
            L = t.shape[-2]
            half = D // 2
            freqs = 1.0 / theta ** (jnp.arange(half, dtype=jnp.float32) / half)
            angles = scale * jnp.arange(L, dtype=jnp.float32)[:, None] * freqs[None, :]
            cos = jnp.cos(angles)
            sin = jnp.sin(angles)
            t1, t2 = (t[..., :half], t[..., half:])
            return jnp.concatenate([t1 * cos - t2 * sin, t1 * sin + t2 * cos], axis=-1)
        key = jax.random.key(seed)
        k1, k2, k3 = jax.random.split(key, 3)
        B, L, Dm = (2, 512, 128)
        x = jax.random.normal(k1, (B, L, Dm), dtype=jnp.float32)
        w_qkv = jax.random.normal(k2, (Dm, 3 * Dm), dtype=jnp.float32) * (1.0 / math.sqrt(Dm))
        b_qkv = jnp.zeros((3 * Dm,), dtype=jnp.float32)
        w_out = jax.random.normal(k3, (Dm, Dm), dtype=jnp.float32) * (1.0 / math.sqrt(Dm))
        b_out = jnp.zeros((Dm,), dtype=jnp.float32)
        return {'x': x, 'w_qkv': w_qkv, 'b_qkv': b_qkv, 'w_out': w_out, 'b_out': b_out}
    _L2_attn_in = _L2_attn_setup()

    def _L2_ffn_setup():
        import jax, jax.numpy as jnp
        import numpy as np
        B, S, D = (1, 256, 128)
        E, K, F = (8, 2, 176)
        NS = 2
        SCALE = 2.5

        def _swiglu_mlp(x, wg, wu, wd):
            return jax.nn.silu(x @ wg) * (x @ wu) @ wd
        key = jax.random.key(seed)
        ks = jax.random.split(key, 8)
        s = 0.02
        return {'hidden_states': jax.random.normal(ks[0], (B, S, D), jnp.float32), 'gate_w': jax.random.normal(ks[1], (E, D), jnp.float32) * s, 'w_gate': jax.random.normal(ks[2], (E, D, F), jnp.float32) * s, 'w_up': jax.random.normal(ks[3], (E, D, F), jnp.float32) * s, 'w_down': jax.random.normal(ks[4], (E, F, D), jnp.float32) * s, 'sw_gate': jax.random.normal(ks[5], (D, F * NS), jnp.float32) * s, 'sw_up': jax.random.normal(ks[6], (D, F * NS), jnp.float32) * s, 'sw_down': jax.random.normal(ks[7], (F * NS, D), jnp.float32) * s}
    _L2_ffn_in = _L2_ffn_setup()

    def _L3_attn_setup():
        import jax, jax.numpy as jnp
        import numpy as np
        MODEL_DIM = 128
        NUM_HEADS = 16
        HEAD_DIM = MODEL_DIM // NUM_HEADS
        ROPE_PERIOD = 10000.0

        def _rope_cos_sin(seq_len, dim, dtype):
            inv_freq = 1.0 / ROPE_PERIOD ** (jnp.arange(0, dim, 2, dtype=jnp.float32) / dim)
            t = jnp.arange(seq_len, dtype=jnp.float32)
            freqs = jnp.outer(t, inv_freq)
            emb = jnp.concatenate([freqs, freqs], axis=-1)
            return (jnp.cos(emb).astype(dtype), jnp.sin(emb).astype(dtype))

        def _rope_embed(x):
            S, D = (x.shape[-2], x.shape[-1])
            cos, sin = _rope_cos_sin(S, D, x.dtype)
            x1 = x[..., :D // 2]
            x2 = x[..., D // 2:]
            rotated = jnp.concatenate([-x2, x1], axis=-1)
            return x * cos + rotated * sin
        key = jax.random.key(seed)
        kx, kq, kk, kv, ko = jax.random.split(key, 5)
        std = 0.02
        return {'x': jax.random.normal(kx, (2, 256, MODEL_DIM), dtype=jnp.float32), 'Wq': std * jax.random.normal(kq, (MODEL_DIM, MODEL_DIM), dtype=jnp.float32), 'Wk': std * jax.random.normal(kk, (MODEL_DIM, MODEL_DIM), dtype=jnp.float32), 'Wv': std * jax.random.normal(kv, (MODEL_DIM, MODEL_DIM), dtype=jnp.float32), 'Wo': std * jax.random.normal(ko, (MODEL_DIM, MODEL_DIM), dtype=jnp.float32)}
    _L3_attn_in = _L3_attn_setup()

    def _L3_ffn_setup():
        import jax, jax.numpy as jnp
        import numpy as np
        B, S, H = (8, 512, 128)
        NAV = 128
        E = 8
        F = 2 * H
        key = jax.random.key(seed)
        ks = jax.random.split(key, 12)

        def w(k, shape, fan_in):
            return jax.random.normal(k, shape, dtype=jnp.float32) / np.sqrt(fan_in)
        return {'hidden_states': jax.random.normal(ks[0], (B, S, H), dtype=jnp.float32), 'Wp1': w(ks[1], (H, NAV), H), 'bp1': jnp.zeros((NAV,), jnp.float32), 'Wp2': w(ks[2], (NAV, E), NAV), 'bp2': jnp.zeros((E,), jnp.float32), 'W1': w(ks[3], (E, H, F), H), 'b1': jnp.zeros((E, F), jnp.float32), 'W2': w(ks[4], (E, F, H), F), 'b2': jnp.zeros((E, H), jnp.float32), 'Wo': w(ks[5], (H, H), H), 'bo': jnp.zeros((H,), jnp.float32)}
    _L3_ffn_in = _L3_ffn_setup()
    _d = {'L0_attn_x': _L0_attn_in['x'], 'L0_attn_Wq': _L0_attn_in['Wq'], 'L0_attn_Wk': _L0_attn_in['Wk'], 'L0_attn_Wv': _L0_attn_in['Wv'], 'L0_attn_Wo': _L0_attn_in['Wo'], 'L0_attn_bo': _L0_attn_in['bo'], 'L0_ffn_gamma1': _L0_ffn_in['gamma1'], 'L0_ffn_Wq': _L0_ffn_in['Wq'], 'L0_ffn_bq': _L0_ffn_in['bq'], 'L0_ffn_Wdown': _L0_ffn_in['Wdown'], 'L0_ffn_bdown': _L0_ffn_in['bdown'], 'L0_ffn_Wup': _L0_ffn_in['Wup'], 'L0_ffn_bup': _L0_ffn_in['bup'], 'L0_ffn_Wo': _L0_ffn_in['Wo'], 'L0_ffn_bo': _L0_ffn_in['bo'], 'L0_ffn_gamma2': _L0_ffn_in['gamma2'], 'L0_ffn_Wg': _L0_ffn_in['Wg'], 'L0_ffn_bg': _L0_ffn_in['bg'], 'L0_ffn_We': _L0_ffn_in['We'], 'L1_attn_qkv_w': _L1_attn_in['qkv_w'], 'L1_attn_qkv_b': _L1_attn_in['qkv_b'], 'L1_attn_out_w': _L1_attn_in['out_w'], 'L1_attn_out_b': _L1_attn_in['out_b'], 'L1_ffn_w_gate': _L1_ffn_in['w_gate'], 'L1_ffn_w_up': _L1_ffn_in['w_up'], 'L1_ffn_w_down': _L1_ffn_in['w_down'], 'L2_attn_w_qkv': _L2_attn_in['w_qkv'], 'L2_attn_b_qkv': _L2_attn_in['b_qkv'], 'L2_attn_w_out': _L2_attn_in['w_out'], 'L2_attn_b_out': _L2_attn_in['b_out'], 'L2_ffn_gate_w': _L2_ffn_in['gate_w'], 'L2_ffn_w_gate': _L2_ffn_in['w_gate'], 'L2_ffn_w_up': _L2_ffn_in['w_up'], 'L2_ffn_w_down': _L2_ffn_in['w_down'], 'L2_ffn_sw_gate': _L2_ffn_in['sw_gate'], 'L2_ffn_sw_up': _L2_ffn_in['sw_up'], 'L2_ffn_sw_down': _L2_ffn_in['sw_down'], 'L3_attn_Wq': _L3_attn_in['Wq'], 'L3_attn_Wk': _L3_attn_in['Wk'], 'L3_attn_Wv': _L3_attn_in['Wv'], 'L3_attn_Wo': _L3_attn_in['Wo'], 'L3_ffn_Wp1': _L3_ffn_in['Wp1'], 'L3_ffn_bp1': _L3_ffn_in['bp1'], 'L3_ffn_Wp2': _L3_ffn_in['Wp2'], 'L3_ffn_bp2': _L3_ffn_in['bp2'], 'L3_ffn_W1': _L3_ffn_in['W1'], 'L3_ffn_b1': _L3_ffn_in['b1'], 'L3_ffn_W2': _L3_ffn_in['W2'], 'L3_ffn_b2': _L3_ffn_in['b2'], 'L3_ffn_Wo': _L3_ffn_in['Wo'], 'L3_ffn_bo': _L3_ffn_in['bo']}
    _x0 = _d['L0_attn_x']
    _d['L0_attn_x'] = jax.random.normal(jax.random.fold_in(jax.random.key(seed), 1), (32, 256, 128), dtype=_x0.dtype)
    del _x0
    return _d

def reference(L0_attn_x, L0_attn_Wq, L0_attn_Wk, L0_attn_Wv, L0_attn_Wo, L0_attn_bo, L0_ffn_gamma1, L0_ffn_Wq, L0_ffn_bq, L0_ffn_Wdown, L0_ffn_bdown, L0_ffn_Wup, L0_ffn_bup, L0_ffn_Wo, L0_ffn_bo, L0_ffn_gamma2, L0_ffn_Wg, L0_ffn_bg, L0_ffn_We, L1_attn_qkv_w, L1_attn_qkv_b, L1_attn_out_w, L1_attn_out_b, L1_ffn_w_gate, L1_ffn_w_up, L1_ffn_w_down, L2_attn_w_qkv, L2_attn_b_qkv, L2_attn_w_out, L2_attn_b_out, L2_ffn_gate_w, L2_ffn_w_gate, L2_ffn_w_up, L2_ffn_w_down, L2_ffn_sw_gate, L2_ffn_sw_up, L2_ffn_sw_down, L3_attn_Wq, L3_attn_Wk, L3_attn_Wv, L3_attn_Wo, L3_ffn_Wp1, L3_ffn_bp1, L3_ffn_Wp2, L3_ffn_bp2, L3_ffn_W1, L3_ffn_b1, L3_ffn_W2, L3_ffn_b2, L3_ffn_Wo, L3_ffn_bo):

    def _L0_attn_ref(x, Wq, Wk, Wv, Wo, bo):
        import jax, jax.numpy as jnp
        import numpy as np
        EMBED = 128
        HEADS = 16
        N, S, E = x.shape
        H = HEADS
        Dh = E // 2 // H
        scale = float(E // H) ** 0.5
        left = x[..., :E // 2]
        q = (left @ Wq.T).reshape(N, S, H, Dh)
        k = (left @ Wk.T).reshape(N, S, H, Dh)
        v = (left @ Wv.T).reshape(N, S, H, Dh)
        energy = jnp.einsum('nqhd,nkhd->nqkh', q, k)
        att = jax.nn.softmax(energy / scale, axis=2)
        out = jnp.einsum('nqkh,nkhd->nqhd', att, v)
        out = out.reshape(N, S, E // 2)
        return out @ Wo.T + bo

    def _L0_ffn_ref(x, gamma1, Wq, bq, Wdown, bdown, Wup, bup, Wo, bo, gamma2, Wg, bg, We):
        import jax, jax.numpy as jnp
        import numpy as np
        D = 128
        H = 16
        HD = D // H
        L = 64
        E = 8
        B, T = (4, 256)
        EPS = 1e-06

        def _glorot(k, shape):
            fan_in, fan_out = (shape[-2], shape[-1])
            lim = np.sqrt(6.0 / (fan_in + fan_out)).astype(np.float32)
            return jax.random.uniform(k, shape, jnp.float32, -lim, lim)

        def _rmsnorm(x, gamma):
            return gamma * x * jax.lax.rsqrt(jnp.mean(x * x, axis=-1, keepdims=True) + EPS)
        b, t = (x.shape[0], x.shape[1])
        h = _rmsnorm(x, gamma1)
        q = (h @ Wq + bq).reshape(b, t, H, HD)
        kv = ((h @ Wdown + bdown) @ Wup + bup).reshape(b, t, H, 2 * HD)
        k, v = jnp.split(kv, 2, axis=-1)
        att = jnp.einsum('bthd,btgd->bthg', q, k) / np.sqrt(HD).astype(np.float32)
        att = jax.nn.softmax(att, axis=-1)
        out = jnp.einsum('bthg,btgd->bthd', att, v).reshape(b, t, D)
        x = x + (out @ Wo + bo)
        h2 = _rmsnorm(x, gamma2)
        gate = jax.nn.softmax(h2 @ Wg + bg, axis=-1)
        combined = jnp.einsum('btd,edf,bte->btf', h2, We, gate)
        return x + combined

    def _L1_attn_ref(x, qkv_w, qkv_b, out_w, out_b):
        import jax, jax.numpy as jnp
        import numpy as np
        D = 128
        H = 16
        HD = D // H
        B = 2
        T = 256

        def _apply_rotary(x, rope):
            x1, x2 = (x[..., ::2], x[..., 1::2])
            sin, cos = (rope[..., ::2], rope[..., 1::2])
            return jnp.concatenate([x1 * cos - x2 * sin, x1 * sin + x2 * cos], axis=-1)
        Bx, Tx, Dm = x.shape
        qkv = (x @ qkv_w + qkv_b).reshape(Bx, Tx, 3, H, HD).transpose(2, 0, 3, 1, 4)
        q, k, v = (qkv[0], qkv[1], qkv[2])
        inv_freq = 1.0 / 10000.0 ** (jnp.arange(0, HD, 2, dtype=jnp.float32) / HD)
        t = jnp.arange(Tx, dtype=jnp.float32)
        freqs = t[:, None] * inv_freq[None, :]
        rope = jnp.concatenate([jnp.sin(freqs), jnp.cos(freqs)], axis=-1)
        q = _apply_rotary(q, rope)
        k = _apply_rotary(k, rope)
        scale = HD ** (-0.5)
        scores = jnp.einsum('bhqd,bhkd->bhqk', q, k) * scale
        causal_mask = jnp.triu(jnp.ones((Tx, Tx), dtype=bool), 1)
        scores = jnp.where(causal_mask, -jnp.inf, scores)
        attn = jax.nn.softmax(scores, axis=-1)
        out = jnp.einsum('bhqk,bhkd->bhqd', attn, v)
        out = out.transpose(0, 2, 1, 3).reshape(Bx, Tx, Dm)
        return out @ out_w + out_b

    def _L1_ffn_ref(x, w_gate, w_up, w_down):
        import jax, jax.numpy as jnp
        import numpy as np
        DIM = 128
        HIDDEN = 384
        SCALE = 1.0 / 127.0

        def _dequant(w_int, dtype):
            return w_int.astype(dtype) * jnp.asarray(SCALE, dtype)
        wg = _dequant(w_gate, x.dtype)
        wu = _dequant(w_up, x.dtype)
        wd = _dequant(w_down, x.dtype)
        gate = jnp.einsum('bsd,hd->bsh', x, wg)
        up = jnp.einsum('bsd,hd->bsh', x, wu)
        h = jax.nn.silu(gate) * up
        return jnp.einsum('bsh,dh->bsd', h, wd)

    def _L2_attn_ref(x, w_qkv, b_qkv, w_out, b_out):
        import jax, jax.numpy as jnp
        import numpy as np
        import math
        THETA = 500.0
        SCALE = 1.0
        NUM_HEADS = 16

        def apply_rope(t, theta=THETA, scale=SCALE):
            D = t.shape[-1]
            L = t.shape[-2]
            half = D // 2
            freqs = 1.0 / theta ** (jnp.arange(half, dtype=jnp.float32) / half)
            angles = scale * jnp.arange(L, dtype=jnp.float32)[:, None] * freqs[None, :]
            cos = jnp.cos(angles)
            sin = jnp.sin(angles)
            t1, t2 = (t[..., :half], t[..., half:])
            return jnp.concatenate([t1 * cos - t2 * sin, t1 * sin + t2 * cos], axis=-1)
        B, L, Dm = x.shape
        H = NUM_HEADS
        Dh = Dm // H
        qkv = x @ w_qkv + b_qkv
        qkv = qkv.reshape(B, L, 3, H, Dh)
        qkv = jnp.swapaxes(qkv, 1, 3)
        q, k, v = (qkv[:, :, 0], qkv[:, :, 1], qkv[:, :, 2])
        q = apply_rope(q)
        k = apply_rope(k)
        scale = 1.0 / math.sqrt(Dh)
        w = jnp.einsum('bhqd,bhkd->bhqk', q, k * scale)
        w = jax.nn.softmax(w, axis=-1)
        o = jnp.einsum('bhqk,bhkd->bhqd', w, v)
        o = jnp.swapaxes(o, 1, 2).reshape(B, L, H * Dh)
        return o @ w_out + b_out

    def _L2_ffn_ref(hidden_states, gate_w, w_gate, w_up, w_down, sw_gate, sw_up, sw_down):
        import jax, jax.numpy as jnp
        import numpy as np
        B, S, D = (1, 256, 128)
        E, K, F = (8, 2, 176)
        NS = 2
        SCALE = 2.5

        def _swiglu_mlp(x, wg, wu, wd):
            return jax.nn.silu(x @ wg) * (x @ wu) @ wd
        identity = hidden_states
        x = hidden_states.reshape(-1, hidden_states.shape[-1])
        T = x.shape[0]
        logits = x.astype(jnp.float32) @ gate_w.astype(jnp.float32).T
        scores = jax.nn.softmax(logits, axis=-1)
        topk_w, topk_i = jax.lax.top_k(scores, K)
        topk_w = topk_w / (topk_w.sum(-1, keepdims=True) + 1e-20) * SCALE
        combine = jnp.zeros((T, E), jnp.float32).at[jnp.arange(T)[:, None], topk_i].set(topk_w)
        g = jax.nn.silu(jnp.einsum('td,edf->etf', x, w_gate)) * jnp.einsum('td,edf->etf', x, w_up)
        expert_out = jnp.einsum('etf,efd->etd', g, w_down)
        y = jnp.einsum('te,etd->td', combine, expert_out).astype(x.dtype)
        y = y.reshape(identity.shape)
        return y + _swiglu_mlp(identity, sw_gate, sw_up, sw_down)

    def _L3_attn_ref(x, Wq, Wk, Wv, Wo):
        import jax, jax.numpy as jnp
        import numpy as np
        MODEL_DIM = 128
        NUM_HEADS = 16
        HEAD_DIM = MODEL_DIM // NUM_HEADS
        ROPE_PERIOD = 10000.0

        def _rope_cos_sin(seq_len, dim, dtype):
            inv_freq = 1.0 / ROPE_PERIOD ** (jnp.arange(0, dim, 2, dtype=jnp.float32) / dim)
            t = jnp.arange(seq_len, dtype=jnp.float32)
            freqs = jnp.outer(t, inv_freq)
            emb = jnp.concatenate([freqs, freqs], axis=-1)
            return (jnp.cos(emb).astype(dtype), jnp.sin(emb).astype(dtype))

        def _rope_embed(x):
            S, D = (x.shape[-2], x.shape[-1])
            cos, sin = _rope_cos_sin(S, D, x.dtype)
            x1 = x[..., :D // 2]
            x2 = x[..., D // 2:]
            rotated = jnp.concatenate([-x2, x1], axis=-1)
            return x * cos + rotated * sin
        B, S, Dm = x.shape
        H, Dh = (NUM_HEADS, HEAD_DIM)
        q = (x @ Wq.T).reshape(B, S, H, Dh).transpose(0, 2, 1, 3)
        k = (x @ Wk.T).reshape(B, S, H, Dh).transpose(0, 2, 1, 3)
        v = (x @ Wv.T).reshape(B, S, H, Dh).transpose(0, 2, 1, 3)
        q = _rope_embed(q)
        k = _rope_embed(k)
        scores = jnp.einsum('bhqd,bhkd->bhqk', q, k) / jnp.sqrt(jnp.asarray(Dh, x.dtype))
        neg_inf = jnp.finfo(x.dtype).min
        causal = jnp.triu(jnp.full((S, S), neg_inf, dtype=x.dtype), k=1)
        scores = scores + causal
        attn = jax.nn.softmax(scores, axis=-1)
        out = jnp.einsum('bhqk,bhkd->bhqd', attn, v)
        out = out.transpose(0, 2, 1, 3).reshape(B, S, Dm)
        return out @ Wo.T

    def _L3_ffn_ref(hidden_states, Wp1, bp1, Wp2, bp2, W1, b1, W2, b2, Wo, bo):
        import jax, jax.numpy as jnp
        import numpy as np
        B, S, H = (8, 512, 128)
        NAV = 128
        E = 8
        F = 2 * H
        last = hidden_states[:, -1, :]
        logits = jax.nn.gelu(last @ Wp1 + bp1, approximate=False) @ Wp2 + bp2
        action_probs = jax.nn.softmax(logits, axis=-1)
        sel = jnp.argmax(action_probs, axis=-1)
        w1 = W1[sel]
        w2 = W2[sel]
        h = jax.nn.gelu(jnp.einsum('bsh,bhf->bsf', hidden_states, w1) + b1[sel][:, None, :], approximate=False)
        reasoned = jnp.einsum('bsf,bfh->bsh', h, w2) + b2[sel][:, None, :]
        out = reasoned @ Wo + bo
        return hidden_states + 0.3 * out
    x = L0_attn_x
    xn = _layernorm(x, axis=-1)
    x = x + _L0_attn_ref(xn, L0_attn_Wq, L0_attn_Wk, L0_attn_Wv, L0_attn_Wo, L0_attn_bo) + _L0_ffn_ref(xn, L0_ffn_gamma1, L0_ffn_Wq, L0_ffn_bq, L0_ffn_Wdown, L0_ffn_bdown, L0_ffn_Wup, L0_ffn_bup, L0_ffn_Wo, L0_ffn_bo, L0_ffn_gamma2, L0_ffn_Wg, L0_ffn_bg, L0_ffn_We)
    xn = _layernorm(x, axis=-1)
    x = x + _L1_attn_ref(xn, L1_attn_qkv_w, L1_attn_qkv_b, L1_attn_out_w, L1_attn_out_b) + _L1_ffn_ref(xn, L1_ffn_w_gate, L1_ffn_w_up, L1_ffn_w_down)
    xn = _layernorm(x, axis=-1)
    x = x + _L2_attn_ref(xn, L2_attn_w_qkv, L2_attn_b_qkv, L2_attn_w_out, L2_attn_b_out) + _L2_ffn_ref(xn, L2_ffn_gate_w, L2_ffn_w_gate, L2_ffn_w_up, L2_ffn_w_down, L2_ffn_sw_gate, L2_ffn_sw_up, L2_ffn_sw_down)
    xn = _layernorm(x, axis=-1)
    x = x + _L3_attn_ref(xn, L3_attn_Wq, L3_attn_Wk, L3_attn_Wv, L3_attn_Wo) + _L3_ffn_ref(xn, L3_ffn_Wp1, L3_ffn_bp1, L3_ffn_Wp2, L3_ffn_bp2, L3_ffn_W1, L3_ffn_b1, L3_ffn_W2, L3_ffn_b2, L3_ffn_Wo, L3_ffn_bo)
    return x

_drawn_inputs = setup_inputs


def setup_inputs(seed=0):
    import zlib

    import numpy as np

    out = dict(_drawn_inputs(seed))
    spreads = {'L0_attn_bo': (0.0, 0.1),
     'L0_ffn_gamma1': (1.0, 0.2),
     'L0_ffn_bq': (0.0, 0.509),
     'L0_ffn_bdown': (0.0, 0.412),
     'L0_ffn_bup': (0.0, 0.1),
     'L0_ffn_bo': (0.0, 0.1),
     'L0_ffn_gamma2': (1.0, 0.2),
     'L0_ffn_bg': (0.0, 0.475),
     'L1_attn_qkv_b': (0.0, 0.8),
     'L1_attn_out_b': (0.0, 2.0),
     'L2_attn_b_qkv': (0.0, 0.8),
     'L2_attn_b_out': (0.0, 2.0),
     'L3_ffn_bp1': (0.0, 0.8),
     'L3_ffn_bp2': (0.0, 0.8),
     'L3_ffn_b1': (0.0, 2.0),
     'L3_ffn_b2': (0.0, 2.0),
     'L3_ffn_bo': (0.0, 2.0)}
    factors = {'L0_attn_Wq': 8.0,
     'L0_attn_Wk': 8.0,
     'L0_attn_Wv': 8.0,
     'L0_attn_Wo': 8.0,
     'L1_attn_qkv_w': 8.0,
     'L1_attn_out_w': 8.0,
     'L2_attn_w_qkv': 8.0,
     'L2_attn_w_out': 8.0,
     'L2_ffn_gate_w': 8.0,
     'L2_ffn_w_gate': 8.0,
     'L2_ffn_w_up': 8.0,
     'L2_ffn_w_down': 8.0,
     'L2_ffn_sw_gate': 27.775,
     'L2_ffn_sw_up': 25.21,
     'L2_ffn_sw_down': 25.149,
     'L3_attn_Wq': 64.0,
     'L3_attn_Wk': 64.0,
     'L3_attn_Wv': 64.0,
     'L3_attn_Wo': 64.0,
     'L3_ffn_Wp1': 8.0,
     'L3_ffn_Wp2': 8.0,
     'L3_ffn_W1': 8.0,
     'L3_ffn_W2': 8.0,
     'L3_ffn_Wo': 8.0}
    for name, (base, spread) in spreads.items():
        noise = np.random.default_rng([zlib.crc32(name.encode()), seed]).standard_normal(out[name].shape)
        drawn = base * np.exp(spread * noise) if base else spread * noise
        out[name] = jnp.asarray(drawn.astype(out[name].dtype))
    for name, factor in factors.items():
        out[name] = (out[name] * factor).astype(out[name].dtype)
    return out
```

```python
from contextlib import ExitStack

import numpy as np

import concourse.bass as bass
from concourse import mybir

F32 = mybir.dt.float32
BF16 = mybir.dt.bfloat16
I32 = mybir.dt.int32
U32 = mybir.dt.uint32
ALU = mybir.AluOpType
ACT = mybir.ActivationFunctionType
AX = mybir.AxisListType

NB, S, D = 32, 256, 128
P = 128
BLK = S // P
H, HD = 16, 8
PARTS = 3
SLOTS = PARTS * PARTS
ROW_MAX = P - 2
KM, KE = ROW_MAX, P
RING = 3
TILE = 1024
BANK = 512
SCALE = float(1.0 / np.sqrt(np.float32(HD)))
E8 = 8
MASKED = -1e30
LAYERS = 4
DMA = 16


def columns(fields):
    at, out = 0, {}
    for name, n in fields:
        out[name] = (at, at + n)
        at += n
    return out, at


CONST, CONST_N = columns([("ident", P), ("ones", 4 * 32), ("iota", E8), ("neghalf", 4)])
CONSTB, CONSTB_N = columns([("ident", P), ("maskM", 2 * P), ("maskE", 2 * P)])
ROPE_W = [("q1", D), ("q2", D), ("k1", D), ("k2", D), ("cos", S), ("sin", S), ("bq1", 1), ("bq2", 1),
          ("bk1", 1), ("bk2", 1)]
ATTN_W = [("v", D), ("bv", BLK * D), ("o", D), ("bo", BLK * D)]
L0_W = [("q1", D), ("k1", D)] + ATTN_W + [
    ("qkv2", 3 * D), ("down", D), ("up", 2 * D), ("bdown", D), ("bup", 2 * D), ("bqkv2", 3 * D), ("g1", 1), ("g2", 1),
    ("o2", D), ("bo2", BLK * D), ("gate", E8), ("bgate", E8), ("experts", E8 * D)]
HID1 = 384 // P
L1_W = ROPE_W + ATTN_W + [("ffn", 3 * HID1 * P)]
CH2 = 15
L2_W = ROPE_W + ATTN_W + [("router", E8), ("gate", CH2 * P), ("up", CH2 * P), ("down", E8 * D), ("downr", E8 * D),
                          ("shared", 3 * D)]
EXP3 = 256 + 256 + 2 + 1
L3_W = ROPE_W + ATTN_W + [("p1", P), ("bp1", 1), ("p2", E8), ("bp2", E8), ("experts", E8 * EXP3), ("o3", D)]
WEIGHTS = [columns(w) for w in (L0_W, L1_W, L2_W, L3_W)]
CAUSAL = [False, True, False, True]

ORDER = [
    "E0 E1 E2 F0 E3 F1 E4 F2 E5 F3 E6 E7 V F4 M0 M1 F5 M2 A0 M3 A1 M4 Y M5 M6 M7 T0 A3 A2",
    "F0 F1 E0 E1 E2 E3 M0 E4 M1 E5 M2 V A0 M3 A1 M4 M5 Y T0 A2",
    "F0 F1 F2 F3 F4 F5 F6 F7 E0 E1 M0 E2 M1 E3 M2 E4 M3 E5 M4 E6 M5 E7 M6 V M7 A0 Y F8 T0 A1 F9 A2",
    "F0 E0 R0 E1 F1 E2 E3 M0 E4 M1 E5 M2 V A0 M3 A1 M4 M5 Y T0 A2",
]
AHEAD = {"A": 2, "M": 1, "R": 1, "T": 1, "E": 0, "F": 0, "V": 0, "Y": 0}


class Names:
    pass


def need(engine, sem, count):
    if isinstance(count, int) and count <= 0:
        return
    engine.wait_ge(sem, count)


def worked_out(engine, *counts):
    return [n if isinstance(n, int) else engine.to_reg(n) for n in counts]


def works(n, batches_ahead):
    return not isinstance(n, int) or 0 <= n + batches_ahead < NB


def steps(engine, step):
    for n in range(-2, 4):
        step(n, n % 2)
    with engine.Fori(2, NB // 2 - 2) as pair:
        step(pair * 2, 0)
        step(pair * 2 + 1, 1)
    for n in range(NB - 4, NB):
        step(n, n % 2)


class Ring:

    def __init__(self, order):
        tiles = [(piece[0], int(piece[1:])) for piece in order.split() if len(piece) > 1]
        self.lay(tiles, 0)
        self.per_step = self.held
        self.steps = {}
        start = [0] * RING
        for n in range(-2, NB):
            places = self.lay([t for t in tiles if works(n, AHEAD[t[0]])], start)
            self.steps[n] = places
            start = self.held

    def lay(self, tiles, start):
        held, places = list(start or [0] * RING), {}
        for at, tile in enumerate(tiles):
            s = at % RING
            places[tile] = (s, held[s])
            held[s] += 1
        self.held = held
        return places

    def at(self, m, name, k):
        if isinstance(m, int):
            return self.steps[m - AHEAD[name]][name, k]
        slot, before = self.steps[0][name, k]
        return slot, (m - AHEAD[name]) * self.per_step[slot] + before


def build(nc, x_in_dram, weights_dram, ints_dram, const_dram, constb_dram, out_dram, layers=LAYERS):
    with ExitStack() as ctx:
        def sb(name, shape, dt=F32):
            return ctx.enter_context(nc.sbuf_tensor(name, shape, dt))

        def psum(name, shape):
            return ctx.enter_context(nc.psum_tensor(name, shape, F32))

        def sem(name):
            return ctx.enter_context(nc.semaphore(name))

        ring = [psum(f"ring{i}", [P, TILE]) for i in range(RING)]
        pOZ = psum("pOZ", [P, BANK])
        pY = psum("pY", [P, BANK])

        const = sb("const_sb", [P, CONST_N])
        constb = sb("constb_sb", [P, CONSTB_N], BF16)
        even = max(WEIGHTS[0][1], WEIGHTS[2][1])
        odd = max(WEIGHTS[1][1], WEIGHTS[3][1])
        w_sb = [sb("w_even", [P, even]), sb("w_odd", [P, odd])]
        xres = sb("xres", [P, NB, S])
        B = Names()
        B.ring = ring
        B.pOZ = pOZ
        B.pY = pY
        B.x = sb("x", [P, 2, S])
        B.stats = sb("stats", [P, BLK, 6])
        B.mv = sb("mv", [P, BLK, 2])
        B.ve = sb("ve", [P, BLK])
        B.rstd = sb("rstd", [P, BLK])
        B.xn = sb("xn", [P, 2, S])
        B.xb = sb("xb", [P, 2, S])
        B.xnT = sb("xnT", [P, 2, S])
        B.rt = sb("rt", [P, 4, S])
        B.qk = sb("qk", [P, 2, S])
        B.res = sb("res", [P, 2, S])
        B.parts = sb("parts", [P, 2, 2, PARTS, S], BF16)
        B.QS = [sb(f"QS{i}", [P, H, S], BF16) for i in range(2)]
        B.KS = [sb(f"KS{i}", [P, H, S], BF16) for i in range(2)]
        B.V = sb("V", [P, 2, BLK, H * 32])
        B.prob = sb("prob", [P, 2, TILE])
        B.nm = sb("nm", [P, BLK, H])
        B.nms = sb("nms", [P, BLK, 2, H], BF16)
        B.nmT = sb("nmT", [32, 2, S], BF16)
        B.rz = sb("rz", [P, S])
        B.on = sb("on", [P, S])
        B.xo = sb("xo", [P, 2, S])
        B.acc = sb("acc", [P, BLK, D])
        B.g = sb("g", [P, CH2, S])
        B.sg = sb("sg", [P, 2, BANK])
        B.tok = sb("tok", [P, 2, BLK, 3 * D])
        B.prod1 = sb("prod1", [P, H * H * HD])
        B.am = sb("am", [P, BLK, H])
        B.mix = sb("mix", [P, 2, S])
        B.ss = sb("ss", [P, 2, BLK])
        B.sv = sb("sv", [P, 2, BLK])
        B.r1 = sb("r1", [P, 2, BLK])
        B.r2 = sb("r2", [P, BLK])
        B.ss2 = sb("ss2", [P, BLK])
        B.gl = sb("gl", [P, BLK, E8])
        B.gs = sb("gs", [P, BLK])
        B.comb = sb("comb", [P, 2, BLK, E8])
        B.top = sb("top", [P, BLK, E8])
        B.idx = sb("idx", [P, BLK, E8], U32)
        B.idxf = sb("idxf", [P, BLK, 2])
        B.wt = sb("wt", [P, BLK, 2])
        B.one = sb("one", [P, BLK, E8])
        B.sel_h = sb("sel_h", [P, 1])
        B.sel_g = sb("sel_g", [P, 1])
        B.sel = sb("sel", [1, 4 * E8])
        B.sel_i = sb("sel_i", [1, E8], U32)
        B.wsel = sb("wsel", [P, 2, EXP3])
        B.sq, B.mixT, B.x1T, B.xx = B.sg[:, 0, 0:S], B.sg[:, 0, S:2 * S], B.sg[:, 1, 0:S], B.sg[:, 1, S:2 * S]
        B.x1b, B.x1, B.att, B.rT = B.rt[:, 0:2, :], B.rt[:, 2, :], B.qk, B.sg[:, 0, 0:S]
        B.prod = [B.g[:, 0:8, :].rearrange("p a t -> p (a t)"), B.prod1[:, :]]
        c = lambda name: const[:, CONST[name][0]:CONST[name][1]]
        cb = lambda name: constb[:, CONSTB[name][0]:CONSTB[name][1]]
        ident, identb = c("ident"), cb("ident")
        B.staged = B.g[:, 0:3, :].rearrange("p a t -> p (a t)")[:, 0:CONSTB_N]

        consts_loaded = sem("consts_loaded")
        cleared = sem("cleared")
        constb_ready = sem("constb_ready")
        w_loaded = [sem(f"w_loaded{i}") for i in range(layers)]

        block = ctx.enter_context(nc.Block())
        layer_state = []
        for l in range(layers):
            q = f"L{l}_"
            TE = 6 if CAUSAL[l] else 8
            L = Names()
            L.l = l
            L.causal = CAUSAL[l]
            L.rope = l > 0
            L.TE = TE
            L.tile_full = [sem(f"{q}tile_full{i}") for i in range(RING)]
            L.tile_read = [sem(f"{q}tile_read{i}") for i in range(RING)]
            L.x_loaded = sem(q + "x_loaded")
            L.ln_stats = sem(q + "ln_stats")
            L.ln_var = sem(q + "ln_var")
            L.rstd_ready = sem(q + "rstd_ready")
            L.xn_ready = sem(q + "xn_ready")
            L.xb_ready = sem(q + "xb_ready")
            L.hi_ready = sem(q + "hi_ready")
            L.mid_ready = sem(q + "mid_ready")
            L.parts_ready = sem(q + "parts_ready")
            L.stacked = sem(q + "stacked")
            L.max_split = sem(q + "max_split")
            L.max_placed = sem(q + "max_placed")
            L.pv_done = sem(q + "pv_done")
            L.rz_ready = sem(q + "rz_ready")
            L.on_ready = sem(q + "on_ready")
            L.y_full = sem(q + "y_full")
            L.residual_done = sem(q + "residual_done")
            L.x_stored = sem(q + "x_stored")
            L.prepared = sem(q + "prepared")
            if l > 0:
                L.qk_ready, L.res_ready = sem(q + "qk_ready"), sem(q + "res_ready")
            if l in (0, 3):
                L.pool_sum = sem(q + "pool_sum")
            if l in (0, 2):
                L.experts_summed = sem(q + "experts_summed")
                L.router, L.router_exp, L.router_in = sem(q + "router"), sem(q + "router_exp"), sem(q + "router_in")
                L.gate_ready = sem(q + "gate_ready")
            if l == 0:
                L.sq_ready, L.sv_ready, L.r_ready = sem(q + "sq_ready"), sem(q + "sv_ready"), sem(q + "r_ready")
                L.tok_ready, L.prod_ready, L.prod_read = sem(q + "tok_ready"), sem(q + "prod_ready"), sem(q + "prod_read")
                L.token, L.att_in, L.att_exp = sem(q + "token"), sem(q + "att_in"), sem(q + "att_exp")
                L.att_ready, L.xx_ready = sem(q + "att_ready"), sem(q + "xx_ready")
                L.sq2_ready, L.sv2_ready, L.r2_ready = sem(q + "sq2_ready"), sem(q + "sv2_ready"), sem(q + "r2_ready")
            if l in (1, 2):
                L.gated = sem(q + "gated")
            if l == 3:
                L.gelu_ready, L.choice, L.choice_in = sem(q + "gelu_ready"), sem(q + "choice"), sem(q + "choice_in")
                L.choice_exp, L.choice_ready, L.chosen = sem(q + "choice_exp"), sem(q + "choice_ready"), sem(q + "chosen")
                L.r_ready = sem(q + "r_ready")
            L.ring = Ring(ORDER[l])
            fields = WEIGHTS[l][0]
            L.w = (lambda fields, l: lambda name, a=0, b=None: w_sb[l % 2][
                :, fields[name][0] + a:fields[name][0] + b if b is not None else fields[name][1]])(fields, l)
            layer_state.append(L)

        def full(engine, L, m, name, k):
            slot, before = L.ring.at(m, name, k)
            engine.wait_ge(L.tile_full[slot], before + 1)
            return ring[slot], L.tile_read[slot]

        def read(engine, L, m, name, k):
            slot, before = L.ring.at(m, name, k)
            engine.wait_ge(L.tile_read[slot], before + 1)

        dram = Names()
        dram.x, dram.w, dram.ints, dram.out = x_in_dram, weights_dram, ints_dram, out_dram
        dram.const, dram.constb = const_dram, constb_dram
        sync_program(nc, block, B, layer_state, read, dram, const, w_sb, xres, consts_loaded, w_loaded)
        tensor_program(nc, block, B, layer_state, ring, pOZ, pY, c, ident, identb, cb, consts_loaded, cleared, constb_ready, w_loaded, read)
        scalar_program(nc, block, B, layer_state, full, read)
        vector_program(nc, block, B, layer_state, full, read, c, w_loaded, consts_loaded, constb, constb_ready)
        gpsimd_program(nc, block, B, layer_state, read, c, consts_loaded, cleared, w_loaded)


def sync_program(nc, block, B, layer_state, read, dram, const, w_sb, xres, consts_loaded, w_loaded):
    @block.sync
    def _(sp):
        def load_weights(l):
            n = WEIGHTS[l][1]
            if l == 1:
                a, b = WEIGHTS[1][0]["ffn"]
                sp.dma_start(w_sb[1][:, 0:a], dram.w[1][:, 0:a]).then_inc(w_loaded[1], DMA)
                sp.dma_start(w_sb[1][:, a:b].bitcast(I32), dram.ints).then_inc(w_loaded[1], DMA)
            else:
                sp.dma_start(w_sb[l % 2][:, 0:n], dram.w[l]).then_inc(w_loaded[l], DMA)

        sp.dma_start(const[:, :], dram.const).then_inc(consts_loaded, DMA)
        sp.dma_start(B.staged, dram.constb).then_inc(consts_loaded, DMA)
        for L in layer_state:
            l, last = L.l, L.l == len(layer_state) - 1

            def load(m, p):
                xb_count, loaded_count = worked_out(sp, m - 1, DMA * m)
                need(sp, L.xb_ready, xb_count)
                need(sp, L.x_loaded, loaded_count)
                if l == 0:
                    src = dram.x[bass.ts(m, S), :].rearrange("(b p) d -> p b d", p=P)
                    sp.dma_start(B.x[:, p, :].rearrange("p (b d) -> p b d", d=D), src).then_inc(L.x_loaded, DMA)
                else:
                    sp.dma_start(B.x[:, p, :], xres[:, m, :]).then_inc(L.x_loaded, DMA)

            load(0, 0)
            if l == 0:
                load_weights(0)
            if l + 1 < len(layer_state):
                load_weights(l + 1)

            def stack(p, part):
                for s in range(SLOTS):
                    rows = slice(HD * s, HD * s + HD)
                    if s // PARTS == part:
                        sp.dma_start(B.QS[p][rows, :, :], B.parts[:, p, 0, part, :]).then_inc(L.stacked, DMA)
                    if s % PARTS == part:
                        sp.dma_start(B.KS[p][rows, :, :], B.parts[:, p, 1, part, :]).then_inc(L.stacked, DMA)

            def step(n, p):
                if works(n, 3):
                    load(n + 3, 1 - p)
                if works(n, 2):
                    m = n + 2
                    ready_count, pv_count = worked_out(sp, m + 1, (m - 1) * L.TE)
                    need(sp, L.pv_done, pv_count)
                    sp.wait_ge(L.hi_ready, ready_count)
                    stack(p, 0)
                if works(n, 1):
                    read(sp, L, n + 1, "T", 0)
                    for part in range(2):
                        sp.dma_start(B.QS[1 - p][ROW_MAX + part:ROW_MAX + part + 1, :, :],
                                     B.nmT[H * part:H * part + H, 1 - p, :]).then_inc(L.max_placed, DMA)
                if works(n, 2):
                    (ready_count,) = worked_out(sp, n + 3)
                    sp.wait_ge(L.mid_ready, ready_count)
                    stack(p, 1)
                    sp.wait_ge(L.parts_ready, ready_count)
                    stack(p, 2)
                if works(n, 0):
                    done_count, stored_count = worked_out(sp, n + 1, DMA * n)
                    sp.wait_ge(L.residual_done, done_count)
                    need(sp, L.x_stored, stored_count)
                    if last:
                        dst = dram.out[bass.ts(n, S), :].rearrange("(b p) d -> p b d", p=P)
                        sp.dma_start(dst, B.xo[:, p, :].rearrange("p (b d) -> p b d", d=D)).then_inc(L.x_stored, DMA)
                    else:
                        sp.dma_start(xres[:, n, :], B.xo[:, p, :]).then_inc(L.x_stored, DMA)

            steps(sp, step)
            sp.wait_ge(L.x_stored, NB * DMA)


def m_tiles(causal):
    if causal:
        return [(0, 8 * t, 8, P) for t in range(2)] + [(1, 4 * t, 4, S) for t in range(4)]
    return [(b, 4 * t, 4, S) for b in range(BLK) for t in range(4)]


def e_tiles(causal):
    group = lambda j: [4 * i + j for i in range(4)]
    if causal:
        return [(0, group(j), 0, S) for j in range(4)] + [(1, group(j) + group(j + 1), P, P) for j in (0, 2)]
    return [(b, group(j), 0, S) for b in range(BLK) for j in range(4)]


def tensor_program(nc, block, B, layer_state, ring, pOZ, pY, c, ident, identb, cb, consts_loaded, cleared, constb_ready, w_loaded, read):
    @block.tensor
    def _(pe):
        pe.wait_ge(consts_loaded, 2 * DMA)
        pe.wait_ge(cleared, 5)
        pe.wait_ge(constb_ready, 1)
        for L in layer_state:
            l = L.l
            w = L.w

            def take(m, name, k):
                slot, before = L.ring.at(m, name, k)
                need(pe, L.tile_read[slot], before)
                return ring[slot], L.tile_full[slot]

            def mm(out, lhsT, rhs, start=True, stop=True, loose=False):
                return pe.matmul(out, lhsT, rhs, start=start, stop=stop, skip_group_check=loose)

            def blocks(T, b):
                return T[:, b * P:(b + 1) * P]

            def stage_a(m, q, k):
                xT = B.xnT[:, q, :]
                if k == 0:
                    pe.wait_ge(L.xn_ready, m + 1)
                if k == 1:
                    read(pe, L, m, "A", 0)
                tile, filled = take(m, "A", k)
                if k == 0:
                    for b in range(BLK):
                        t = pe.transpose(tile[:, b * P:(b + 1) * P], B.xn[:, q, b * P:(b + 1) * P], ident)
                if k == 1:
                    for i, name in enumerate(["q1", "q2", "k1", "k2"] if L.rope else ["q1", "k1"]):
                        t = mm(tile[:, i * S:(i + 1) * S], w(name), xT)
                if k == 2:
                    for b in range(BLK):
                        t = mm(tile[:, b * P:(b + 1) * P], blocks(xT, b), w("v"))
                    if l == 2:
                        for b in range(BLK):
                            t = mm(tile[:, BANK + E8 * b:BANK + E8 * b + E8], blocks(xT, b), w("router"))
                    if l == 3:
                        t = mm(tile[:, BANK:BANK + 1], w("p1"), xT[:, S - 1:S])
                if k == 3:
                    for b in range(BLK):
                        t = mm(tile[:, b * BANK:b * BANK + 3 * D], blocks(xT, b), w("qkv2"))
                t.then_inc(filled, 1)

            def stage_m(m, q, k):
                if k == 0:
                    pe.wait_ge(L.stacked, 2 * SLOTS * DMA * m + 2 * SLOTS * DMA)
                b, h0, heads, keys = m_tiles(L.causal)[k]
                tile, filled = take(m, "M", k)
                per_bank = BANK // keys
                for i in range(heads):
                    at = i * keys
                    if L.causal and i % per_bank == 0:
                        diag = tile[:, at:at + BANK].rearrange("p (h k) -> p h k", k=keys)[:, :, keys - P:keys]
                        for j in range(0, per_bank, 2):
                            mm(diag[:, j:j + 2, :], identb, cb("maskM").rearrange("p (h k) -> p h k", k=P),
                               start=j == 0, stop=False, loose=True)
                    t = mm(tile[:, at:at + keys], B.QS[q][0:KM, h0 + i, b * P:(b + 1) * P],
                           B.KS[q][0:KM, h0 + i, 0:keys], start=not L.causal, stop=True, loose=L.causal)
                t.then_inc(filled, 1)

            def stage_t(m, q, k):
                pe.wait_ge(L.max_split, 2 * m + 2)
                tile, filled = take(m, "T", 0)
                for b in range(BLK):
                    t = pe.transpose(tile[0:32, b * 64:(b + 1) * 64].bitcast(BF16),
                                     B.nms[:, b, :, :].rearrange("p a h -> p (a h)"), identb)
                t.then_inc(filled, 1)

            def stage_e(n, p, k):
                if k == 0:
                    pe.wait_ge(L.max_placed, 2 * DMA * n + 2 * DMA)
                scores(n, p, k)
                if k > 0:
                    values(n, p, k - 1)

            def scores(n, p, k):
                b, heads, q0, queries = e_tiles(L.causal)[k]
                tile, filled = take(n, "E", k)
                per_bank = BANK // queries
                for i, h in enumerate(heads):
                    at = i * queries
                    if L.causal and i % per_bank == 0:
                        diag = tile[:, at:at + BANK].rearrange("p (h k) -> p h k", k=queries)[:, :, 0:P]
                        for j in range(0, per_bank, 2):
                            mm(diag[:, j:j + 2, :], identb, cb("maskE").rearrange("p (h k) -> p h k", k=P),
                               start=j == 0, stop=False, loose=True)
                    t = mm(tile[:, at:at + queries], B.KS[p][0:KE, h, b * P:(b + 1) * P],
                           B.QS[p][0:KE, h, q0:q0 + queries], start=not L.causal, stop=True, loose=L.causal)
                t.then_inc(filled, 1)

            def values(n, p, k):
                if k == 0:
                    need(pe, L.on_ready, n)
                b, heads, q0, queries = e_tiles(L.causal)[k]
                read(pe, L, n, "E", k)
                prob = B.prob[:, k % 2, :]
                for o, col in ((0, "v"), (1, "ones")):
                    for i, h in enumerate(heads):
                        g, j = h // 4, h % 4
                        lhsT = B.V[:, p, b, h * 32:h * 32 + 32] if o == 0 else c("ones")[:, 32 * j:32 * j + 32]
                        t = mm(pOZ[32 * g:32 * g + 32, o * S + q0:o * S + q0 + queries], lhsT,
                               prob[:, i * queries:(i + 1) * queries],
                               start=(k == 0 and o == 0), stop=True, loose=True)
                t.then_inc(L.pv_done, 1)


            def attention_out(n, start=True, stop=False):
                pe.wait_ge(L.on_ready, n + 1)
                need(pe, L.residual_done, n)
                for b in range(BLK):
                    t = mm(pY[:, b * D:(b + 1) * D], blocks(B.on, b), w("o"), start=start and b == 0, stop=stop,
                           loose=True)
                return t

            def stage_f0(n, p, k):
                if k == 0:
                    pe.wait_ge(L.prod_read, 4 * n + 4)
                if k in (1, 2, 3):
                    read(pe, L, n, "F", k - 1)
                tile, filled = take(n, "F", k)
                if k >= 4:
                    for half in range(2):
                        t = mm(tile[:, half * BANK:(half + 1) * BANK], blocks(B.x1T, k - 4),
                               w("experts", half * BANK, (half + 1) * BANK))
                else:
                    for b in range(BLK):
                        if k == 0:
                            t = pe.transpose(tile[:, b * P:(b + 1) * P], B.mix[:, p, b * P:(b + 1) * P], ident)
                        if k == 1:
                            t = mm(tile[:, b * P:(b + 1) * P], blocks(B.mixT, b), w("o2"))
                        if k == 2:
                            t = pe.transpose(tile[:, b * P:(b + 1) * P], B.x1[:, b * P:(b + 1) * P], ident)
                        if k == 3:
                            t = mm(tile[:, b * E8:(b + 1) * E8], blocks(B.x1T, b), w("gate"))
                t.then_inc(filled, 1)

            def up_tile(n, p, k, chunks, gate, up):
                tile, filled = take(n, "F", k)
                for half, name, base in ((0, gate, 0), (1, up[0], up[1])):
                    for ch in range(2 * k, min(2 * k + 2, chunks)):
                        t = mm(tile[:, half * BANK + (ch % 2) * S:half * BANK + (ch % 2) * S + S],
                               w(name, base + ch * P, base + (ch + 1) * P), B.xnT[:, p, :])
                t.then_inc(filled, 1)

            def stage_f1(n, p, k):
                up_tile(n, p, k, HID1, "ffn", ("ffn", HID1 * P))

            def stage_f2(n, p, k):
                if k < 8:
                    up_tile(n, p, k, CH2, "gate", ("up", 0))
                    return
                b = k - 8
                tile, filled = take(n, "F", k)
                for e in range(E8):
                    out = tile[:, e * D:(e + 1) * D]
                    mm(out, blocks(B.g[:, e, :], b), w("down", e * D, (e + 1) * D), stop=False)
                    t = mm(out, blocks(B.g[:, E8 + e // 2, :], b), w("downr", e * D, (e + 1) * D), start=False)
                t.then_inc(filled, 1)

            def stage_r(m, q, k):
                pe.wait_ge(L.gelu_ready, m + 1)
                tile, filled = take(m, "R", 0)
                mm(tile[0:1, 0:E8], B.sel_g[:, 0:1], w("p2")).then_inc(filled, 1)

            def stage_f3(n, p, k):
                if k == 0:
                    pe.wait_ge(L.chosen, n + 1)
                else:
                    read(pe, L, n, "F", 0)
                tile, filled = take(n, "F", k)
                for ch in range(2):
                    if k == 0:
                        t = mm(tile[:, ch * S:(ch + 1) * S], B.wsel[:, p, ch * P:(ch + 1) * P], B.xnT[:, p, :])
                    else:
                        t = mm(tile[:, 0:S], B.wsel[:, p, 256 + ch * P:256 + (ch + 1) * P], B.g[:, ch, :],
                               start=ch == 0, stop=ch == 1)
                t.then_inc(filled, 1)

            def output(n):
                t = attention_out(n, stop=l == 0)
                if l == 1:
                    for ch in range(HID1):
                        if ch % 2 == 0:
                            read(pe, L, n, "F", ch // 2)
                        for b in range(BLK):
                            t = mm(pY[:, b * D:(b + 1) * D], blocks(B.g[:, ch, :], b),
                                   w("ffn", (2 * HID1 + ch) * P, (2 * HID1 + ch + 1) * P), start=False,
                                   stop=ch == HID1 - 1, loose=True)
                if l == 2:
                    read(pe, L, n, "F", 7)
                    for s in range(3):
                        for b in range(BLK):
                            t = mm(pY[:, b * D:(b + 1) * D], blocks(B.g[:, 12 + s, :], b),
                                   w("shared", s * D, (s + 1) * D), start=False, stop=s == 2, loose=True)
                if l == 3:
                    read(pe, L, n, "F", 1)
                    for b in range(BLK):
                        t = mm(pY[:, b * D:(b + 1) * D], blocks(B.rT, b), w("o3"), start=False, stop=True, loose=True)
                t.then_inc(L.y_full, 1)

            stage_f = [stage_f0, stage_f1, stage_f2, stage_f3][l]

            def step(n, p):
                for piece in ORDER[l].split():
                    name, k = piece[0], int(piece[1:] or 0)
                    if not works(n, AHEAD[name]):
                        continue
                    m, parity = n + AHEAD[name], (p + AHEAD[name]) % 2
                    if name == "V":
                        values(m, parity, L.TE - 1)
                    elif name == "Y":
                        output(m)
                    else:
                        {"A": stage_a, "M": stage_m, "R": stage_r, "T": stage_t, "E": stage_e, "F": stage_f}[name](m, parity, k)

            if l == 0:
                pe.wait_ge(w_loaded[0], DMA)
                mm(ring[0][:, 0:2 * D], w("down"), w("up"))
                mm(ring[0][:, BANK:BANK + 2 * D], w("bdown"), w("up")).then_inc(L.prepared, 1)
            pe.wait_ge(L.prepared, 2 if l == 0 else 1)
            steps(pe, step)


class Chain:

    def __init__(self, engine, sem, per, m):
        self.engine, self.sem, self.per, self.m, self.i = engine, sem, per, m, 0

    def __call__(self, instruction, constants=None):
        self.i += 1
        assert self.i <= self.per
        instruction.then_inc(self.sem, 1)
        (count,) = worked_out(self.engine, self.m * self.per + self.i)
        if constants is not None:
            self.engine.wait_ge(constants, 2 * DMA)
        self.engine.wait_ge(self.sem, count)


def scalar_program(nc, block, B, layer_state, full, read):
    @block.scalar
    def _(act):
        for L in layer_state:
            l = L.l

            def transposed(m, q):
                tile, done = full(act, L, m, "A", 0)
                if l > 0 and not (isinstance(m, int) and m < 2):
                    read(act, L, m - 2, "F", (0, 1, 7, 0)[l])
                act.activation(B.xnT[:, q, :], tile[:, 0:S], ACT.Copy).then_inc(done, 1)

            def high(m, q):
                if L.rope:
                    act.wait_ge(L.qk_ready, m + 1)
                    src = B.qk[:, :, :]
                else:
                    tile, done = full(act, L, m, "A", 1)
                    src = tile[:, 0:2 * S].rearrange("p (a t) -> p a t", a=2)
                need(act, L.stacked, 2 * SLOTS * DMA * (m - 1))
                act.activation(B.parts[:, q, :, 0, :], src, ACT.Copy).then_inc(L.hi_ready, 1)

            def middle(m, q):
                if L.rope:
                    act.wait_ge(L.res_ready, m + 1)
                else:
                    read(act, L, m, "A", 1)
                act.activation(B.parts[:, q, :, 1, :], B.res[:, :, :], ACT.Copy).then_inc(L.mid_ready, 1)

            def exponentials(n, k):
                tile, done = full(act, L, n, "E", k)
                need(act, L.pv_done, L.TE * n + (k - 1))
                act.activation(B.prob[:, k % 2, :], tile[:, :], ACT.Exp, scale=SCALE).then_inc(done, 1)

            def maximum_transposed(m, q):
                tile, done = full(act, L, m, "T", 0)
                need(act, L.max_placed, 2 * DMA * (m - 1))
                act.activation(B.nmT[:, q, :], tile[0:32, 0:P].bitcast(BF16), ACT.Copy).then_inc(done, 1)

            def copy_tile(n, k, dst):
                tile, done = full(act, L, n, "F", k)
                act.activation(dst, tile[:, 0:S], ACT.Copy).then_inc(done, 1)

            def router_exp(m):
                act.wait_ge(L.router_in, m + 1)
                act.activation(B.gl[:, :, :], B.gl[:, :, :], ACT.Exp).then_inc(L.router_exp, 1)

            def gates(n, chunks, k):
                tile, _ = full(act, L, n, "F", k)
                width = S * min(2, chunks - 2 * k)
                if k >= 2:
                    read(act, L, n, "F", k - 2)
                act.activation(B.sg[:, k % 2, 0:width], tile[:, 0:width], ACT.Silu).then_inc(L.gated, 1)

            def step_0(n, p):
                if works(n, 0):
                    for k in range(3):
                        exponentials(n, k)
                    copy_tile(n, 0, B.mixT[:, :])
                    exponentials(n, 3)
                    exponentials(n, 4)
                    copy_tile(n, 2, B.x1T[:, :])
                    exponentials(n, 5)
                    exponentials(n, 6)
                if works(n, 1):
                    act.wait_ge(L.att_in, n + 2)
                    act.activation(B.att[:, :, :], B.att[:, :, :], ACT.Exp, scale=SCALE).then_inc(L.att_exp, 1)
                if works(n, 0):
                    exponentials(n, 7)
                    router_exp(n)
                if works(n, 2):
                    transposed(n + 2, p)
                    high(n + 2, p)
                    middle(n + 2, p)
                if works(n, 1):
                    maximum_transposed(n + 1, 1 - p)

            def step_1(n, p):
                if works(n, 0):
                    gates(n, HID1, 0)
                    gates(n, HID1, 1)
                    for k in range(L.TE):
                        exponentials(n, k)
                if works(n, 2):
                    transposed(n + 2, p)
                    high(n + 2, p)
                if works(n, 1):
                    maximum_transposed(n + 1, 1 - p)
                if works(n, 2):
                    middle(n + 2, p)

            def step_2(n, p):
                if works(n, 1):
                    router_exp(n + 1)
                if works(n, 0):
                    for k in range(8):
                        gates(n, CH2, k)
                    for k in range(L.TE):
                        exponentials(n, k)
                if works(n, 2):
                    transposed(n + 2, p)
                if works(n, 1):
                    maximum_transposed(n + 1, 1 - p)
                if works(n, 2):
                    high(n + 2, p)
                    middle(n + 2, p)

            def step_3(n, p):
                if works(n, 0):
                    tile, done = full(act, L, n, "F", 0)
                    act.wait_ge(L.chosen, n + 1)
                    for ch in range(2):
                        t = act.activation(B.g[:, ch, :], tile[:, ch * S:(ch + 1) * S], ACT.Gelu,
                                           bias=B.wsel[:, p, 512 + ch:513 + ch])
                    t.then_inc(done, 1)
                if works(n, 1):
                    read(act, L, n + 1, "A", 2)
                    act.activation(B.sel_g[:, 0:1], B.sel_h[:, 0:1], ACT.Gelu).then_inc(L.gelu_ready, 1)
                if works(n, 0):
                    for k in range(3):
                        exponentials(n, k)
                if works(n, 1):
                    act.wait_ge(L.choice_in, n + 2)
                    act.activation(B.sel[0:1, 0:E8], B.sel[0:1, 0:E8], ACT.Exp, bias=B.sel[0:1, 2 * E8:2 * E8 + 1])\
                       .then_inc(L.choice_exp, 1)
                if works(n, 0):
                    for k in range(3, L.TE):
                        exponentials(n, k)
                if works(n, 2):
                    transposed(n + 2, p)
                    high(n + 2, p)
                if works(n, 1):
                    maximum_transposed(n + 1, 1 - p)
                if works(n, 2):
                    middle(n + 2, p)

            step = [step_0, step_1, step_2, step_3][l]
            steps(act, step)


def vector_program(nc, block, B, layer_state, full, read, c, w_loaded, consts_loaded, constb, constb_ready):
    @block.vector
    def _(dve):
        dve.wait_ge(consts_loaded, 2 * DMA)
        dve.tensor_copy(constb[:, :], B.staged).then_inc(constb_ready, 1)
        for L in layer_state:
            l, w = L.l, L.w

            def prepare():
                dve.wait_ge(w_loaded[l], DMA * (2 if l == 1 else 1))
                if l == 0:
                    g1, g2 = w("g1"), w("g2")
                    dve.tensor_scalar(w("qkv2", 0, D), w("qkv2", 0, D), g1, None, ALU.mult)
                    dve.tensor_scalar(w("gate"), w("gate"), g2, None, ALU.mult)
                    dve.tensor_scalar(w("experts"), w("experts"), g2, None, ALU.mult)
                    dve.wait_ge(L.prepared, 1)
                    dve.tensor_scalar(w("qkv2", D, 3 * D), B.ring[0][:, 0:2 * D], g1, None, ALU.mult)
                    t = dve.tensor_tensor(w("bqkv2", D, 3 * D), B.ring[0][:, BANK:BANK + 2 * D], w("bup"), ALU.add)
                elif l == 1:
                    t = dve.tensor_scalar(w("ffn"), w("ffn").bitcast(I32), float(np.float32(1.0 / 127.0)), None, ALU.mult)
                elif l == 2:
                    t = dve.tensor_scalar(w("bo"), w("bo"), 1.0, None, ALU.mult)
                else:
                    t = dve.tensor_scalar(w("bo"), w("bo"), 0.3, None, ALU.mult)
                t.then_inc(L.prepared, 1)

            def ln_stats(m, p):
                dve.wait_ge(L.x_loaded, DMA * m + DMA)
                for b in range(BLK):
                    t = dve.bn_stats(B.stats[:, b, :], B.x[:, p, b * D:(b + 1) * D])
                t.then_inc(L.ln_stats, 1)
                (stats_count,) = worked_out(dve, 2 * m + 1)
                dve.wait_ge(consts_loaded, 2 * DMA)
                dve.wait_ge(L.ln_stats, stats_count)
                for b in range(BLK):
                    t = dve.bn_aggr(B.mv[:, b, :], B.stats[:, b, :])
                t.then_inc(L.ln_stats, 1)

            def ln_apply(m, p):
                dve.wait_ge(L.rstd_ready, m + 1)
                need(dve, L.xb_ready, m - 1)
                for b in range(BLK):
                    t = dve.tensor_scalar(B.xn[:, p, b * D:(b + 1) * D], B.x[:, p, b * D:(b + 1) * D],
                                          B.mv[:, b, 0:1], B.rstd[:, b:b + 1], ALU.subtract, ALU.mult)
                t.then_inc(L.xn_ready, 1)
                if l == 0:
                    dve.wait_ge(L.xn_ready, m + 1)
                    for b in range(BLK):
                        xb = B.xn[:, p, b * D:(b + 1) * D]
                        t = dve.tensor_tensor_reduce(B.sq[:, b * D:(b + 1) * D], xb, xb, 1.0, 0.0, ALU.mult, ALU.add,
                                                     B.ss[:, p, b:b + 1])
                    t.then_inc(L.sq_ready, 1)

            def rotate(m, q):
                tile, done = full(dve, L, m, "A", 1)
                for i, (b, table) in enumerate((("bq1", "cos"), ("bq2", "sin"), ("bk1", "cos"), ("bk2", "sin"))):
                    t = dve.scalar_tensor_tensor(B.rt[:, i, :], tile[:, i * S:(i + 1) * S], w(b), w(table),
                                                 ALU.add, ALU.mult)
                t.then_inc(done, 1)
                read(dve, L, m, "A", 1)
                rt = B.rt[:, :, :].rearrange("p (a r) t -> p a r t", r=2)
                dve.tensor_tensor(B.qk[:, :, :], rt[:, :, 0, :], rt[:, :, 1, :], ALU.add).then_inc(L.qk_ready, 1)

            def remainder(m, q):
                if L.rope:
                    src, ready = B.qk[:, :, :], L.res_ready
                else:
                    tile, ready = full(dve, L, m, "A", 1)
                    src = tile[:, 0:2 * S].rearrange("p (a t) -> p a t", a=2)
                dve.wait_ge(L.hi_ready, m + 1)
                need(dve, L.parts_ready, m)
                dve.tensor_tensor(B.res[:, :, :], src, B.parts[:, q, :, 0, :], ALU.subtract).then_inc(ready, 1)

            def values_in(m, q):
                tile, done = full(dve, L, m, "A", 2)
                need(dve, L.pv_done, L.TE * (m - 1))
                for j in range(4):
                    spread = B.V[:, q, :, :].rearrange("p b (i r) -> p b i r", r=P)[:, :, :, 40 * j:40 * j + HD]
                    v = tile[:, 0:BLK * D].rearrange("p (b i j d) -> p b i j d", b=BLK, i=4, j=4)[:, :, :, j, :]
                    bv = w("bv").rearrange("p (b i j d) -> p b i j d", b=BLK, i=4, j=4)[:, :, :, j, :]
                    t = dve.tensor_tensor(spread, v, bv, ALU.add)
                if l == 2:
                    t = dve.tensor_copy(B.gl[:, :, :], tile[:, BANK:BANK + 2 * E8].rearrange("p (b e) -> p b e", b=BLK))
                if l == 3:
                    t = dve.tensor_scalar(B.sel_h[:, :], tile[:, BANK:BANK + 1], w("bp1"), None, ALU.add)
                t.then_inc(done, 1)

            def token_qkv(m, q):
                tile, done = full(dve, L, m, "A", 3)
                dve.wait_ge(L.r_ready, m + 1)
                for b in range(BLK):
                    t = dve.scalar_tensor_tensor(B.tok[:, q, b, :], tile[:, b * BANK:b * BANK + 3 * D],
                                                 B.r1[:, q, b:b + 1], w("bqkv2"), ALU.mult, ALU.add)
                t.then_inc(done, 1)

            def route_in(m):
                read(dve, L, m, "A", 2)
                chain = Chain(dve, L.router, ROUTE, m)
                chain(dve.tensor_reduce(B.gs[:, :], B.gl[:, :, :], AX.X, ALU.max))
                dve.tensor_tensor(B.gl[:, :, :], B.gl[:, :, :], B.gs[:, :].unsqueeze(2).to_broadcast([P, BLK, E8]),
                                  ALU.subtract).then_inc(L.router_in, 1)

            def route(m, q):
                chain = Chain(dve, L.router, ROUTE, m)
                chain.i = 1
                dve.wait_ge(L.router_exp, m + 1)
                chain(dve.tensor_reduce(B.gs[:, :], B.gl[:, :, :], AX.X, ALU.add))
                chain(dve.reciprocal(B.gs[:, :], B.gs[:, :]))
                chain(dve.tensor_tensor(B.gl[:, :, :], B.gl[:, :, :],
                                        B.gs[:, :].unsqueeze(2).to_broadcast([P, BLK, E8]), ALU.mult), consts_loaded)
                dve.max(B.top[:, 0, :], B.gl[:, 0, :])
                chain(dve.max(B.top[:, 1, :], B.gl[:, 1, :]), consts_loaded)
                dve.max_index(B.idx[:, 0, :], B.top[:, 0, :], B.gl[:, 0, :])
                chain(dve.max_index(B.idx[:, 1, :], B.top[:, 1, :], B.gl[:, 1, :]))
                dve.tensor_copy(B.idxf[:, :, :], B.idx[:, :, 0:2])
                chain(dve.scalar_tensor_tensor(B.gs[:, :], B.top[:, :, 0], 1e-20, B.top[:, :, 1], ALU.add, ALU.add))
                chain(dve.reciprocal(B.gs[:, :], B.gs[:, :]))
                chain(dve.scalar_tensor_tensor(B.wt[:, :, :], B.top[:, :, 0:2], 2.5,
                                               B.gs[:, :].unsqueeze(2).to_broadcast([P, BLK, 2]), ALU.mult, ALU.mult))
                for b in range(BLK):
                    dve.tensor_scalar(B.one[:, b, :], c("iota"), B.idxf[:, b, 0:1], B.wt[:, b, 0:1], ALU.is_equal, ALU.mult)
                    t = dve.tensor_scalar(B.comb[:, q, b, :], c("iota"), B.idxf[:, b, 1:2], B.wt[:, b, 1:2],
                                          ALU.is_equal, ALU.mult)
                chain(t)
                chain(dve.tensor_tensor(B.comb[:, q, :, :], B.comb[:, q, :, :], B.one[:, :, :], ALU.add))

            def normalise(n):
                dve.wait_ge(L.pv_done, L.TE * n + L.TE)
                dve.reciprocal(B.rz[:, :], B.pOZ[:, S:2 * S]).then_inc(L.rz_ready, 1)
                dve.wait_ge(L.rz_ready, n + 1)
                need(dve, L.y_full, n)
                dve.tensor_tensor(B.on[:, :], B.pOZ[:, 0:S], B.rz[:, :], ALU.mult).then_inc(L.on_ready, 1)

            def maxima(m, *ks):
                for k in ks:
                    b, h0, heads, keys = m_tiles(L.causal)[k]
                    tile, done = full(dve, L, m, "M", k)
                    dve.tensor_reduce(B.nm[:, b, h0:h0 + heads], tile[:, :].rearrange("p (h k) -> p h k", k=keys),
                                      AX.X, ALU.max, negate=True).then_inc(done, 1)

            def split_max(m):
                for back in range(1, RING + 1):
                    read(dve, L, m, "M", L.TE - back)
                dve.tensor_copy(B.nms[:, :, 0, :], B.nm[:, :, :]).then_inc(L.max_split, 1)
                dve.wait_ge(L.max_split, 2 * m + 1)
                dve.tensor_tensor(B.nms[:, :, 1, :], B.nm[:, :, :], B.nms[:, :, 0, :], ALU.subtract).then_inc(L.max_split, 1)

            def token_scores(m, b):
                dve.wait_ge(L.prod_ready, 4 * m + b + 1)
                dve.tensor_reduce(B.att[:, b, :], B.prod[b].rearrange("p (a d) -> p a d", d=HD), AX.X, ALU.add)\
                   .then_inc(L.prod_read, 1)

            def token_views():
                att = B.att[:, :, :].rearrange("p b (h g) -> p (b h) g", g=H)
                am = B.am[:, :, :].rearrange("p b h -> p (b h)")
                return att, am, am.unsqueeze(2).to_broadcast([P, BLK * H, H])

            def token_softmax_in(m):
                att, am, spread = token_views()
                chain = Chain(dve, L.token, 3, m)
                dve.wait_ge(L.prod_read, 4 * m + 2)
                chain(dve.tensor_reduce(am, att, AX.X, ALU.max))
                dve.tensor_tensor(att, att, spread, ALU.subtract).then_inc(L.att_in, 1)

            def token_softmax_out(m):
                att, am, spread = token_views()
                chain = Chain(dve, L.token, 3, m)
                chain.i = 1
                dve.wait_ge(L.att_exp, m + 1)
                chain(dve.tensor_reduce(am, att, AX.X, ALU.add))
                chain(dve.reciprocal(am, am))
                dve.tensor_tensor(att, att, spread, ALU.mult).then_inc(L.att_ready, 1)

            def token_mix(n, p, b):
                dve.wait_ge(L.prod_ready, 4 * n + 3 + b)
                dve.tensor_reduce(B.mix[:, p, b * D:(b + 1) * D], B.prod[b].rearrange("p (a g) -> p a g", g=H),
                                  AX.X, ALU.add).then_inc(L.prod_read, 1)

            def sum_experts(n, b, first, weight, base):
                tile, done = full(dve, L, n, "F", first + b)
                for e in range(E8):
                    out, part = tile[:, e * D:(e + 1) * D], (base if e % 2 == 0 else B.acc[:, b, :])
                    if e > 1:
                        dve.wait_ge(L.experts_summed, 15 * n + (7 * b + e - 1))
                    if e == 1:
                        t = dve.tensor_scalar(part, out, weight(e), None, ALU.mult)
                    else:
                        t = dve.scalar_tensor_tensor(part, out, weight(e), part, ALU.mult, ALU.add)
                    t.then_inc(L.experts_summed if e < E8 - 1 else done, 1)

            def combine(n, first, base):
                for b in range(BLK):
                    read(dve, L, n, "F", first + b)
                acc = B.acc[:, :, :].rearrange("p b d -> p (b d)")
                dve.tensor_tensor(acc, acc, base, ALU.add).then_inc(L.experts_summed, 1)
                dve.wait_ge(L.experts_summed, 15 * n + 15)
                return acc

            def residual(n, p, base):
                need(dve, L.x_stored, DMA * (n - 1))
                return dve.tensor_tensor(B.xo[:, p, :], B.pY[:, 0:S], base, ALU.add)

            def x1(n, p):
                tile, done = full(dve, L, n, "F", 1)
                dve.wait_ge(L.xb_ready, n + 1)
                dve.tensor_tensor(B.x1[:, :], tile[:, 0:S], B.x1b[:, p, :], ALU.add).then_inc(done, 1)
                read(dve, L, n, "F", 1)
                for b in range(BLK):
                    xb = B.x1[:, b * D:(b + 1) * D]
                    t = dve.tensor_tensor_reduce(B.sq[:, b * D:(b + 1) * D], xb, xb, 1.0, 0.0, ALU.mult, ALU.add,
                                                 B.ss2[:, b:b + 1])
                t.then_inc(L.sq2_ready, 1)

            def gate_in(n):
                tile, done = full(dve, L, n, "F", 3)
                dve.wait_ge(L.r2_ready, n + 1)
                chain = Chain(dve, L.router, 4, n)
                for b in range(BLK):
                    t = dve.scalar_tensor_tensor(B.gl[:, b, :], tile[:, b * E8:(b + 1) * E8], B.r2[:, b:b + 1],
                                                 w("bgate"), ALU.mult, ALU.add)
                t.then_inc(done, 1)
                read(dve, L, n, "F", 3)
                chain(dve.tensor_reduce(B.gs[:, :], B.gl[:, :, :], AX.X, ALU.max))
                dve.tensor_tensor(B.gl[:, :, :], B.gl[:, :, :], B.gs[:, :].unsqueeze(2).to_broadcast([P, BLK, E8]),
                                  ALU.subtract).then_inc(L.router_in, 1)

            def gate_out(n):
                chain = Chain(dve, L.router, 4, n)
                chain.i = 1
                dve.wait_ge(L.router_exp, n + 1)
                chain(dve.tensor_reduce(B.gs[:, :], B.gl[:, :, :], AX.X, ALU.add))
                chain(dve.reciprocal(B.gs[:, :], B.gs[:, :]))
                chain(dve.tensor_tensor(B.gs[:, :], B.gs[:, :], B.r2[:, :], ALU.mult))
                dve.tensor_tensor(B.gl[:, :, :], B.gl[:, :, :], B.gs[:, :].unsqueeze(2).to_broadcast([P, BLK, E8]),
                                  ALU.mult).then_inc(L.gate_ready, 1)
                dve.wait_ge(L.gate_ready, n + 1)

            def hidden(n, chunks, *ks):
                for k in ks:
                    tile, done = full(dve, L, n, "F", k)
                    width = S * min(2, chunks - 2 * k)
                    dve.wait_ge(L.gated, (chunks + 1) // 2 * n + (k + 1))
                    g = B.g[:, 2 * k:2 * k + width // S, :].rearrange("p a t -> p (a t)")
                    dve.tensor_tensor(g, tile[:, BANK:BANK + width], B.sg[:, k % 2, 0:width], ALU.mult).then_inc(done, 1)

            def choice_views():
                sel = B.sel
                return sel[0:1, 0:E8], sel[0:1, E8:2 * E8], sel[0:1, 2 * E8:2 * E8 + 1], sel[0:1, 3 * E8:3 * E8 + 1]

            def choose_in(m):
                lg, top, small, total = choice_views()
                chain = Chain(dve, L.choice, 5, m)
                tile, done = full(dve, L, m, "R", 0)
                dve.tensor_tensor(lg, tile[0:1, 0:E8], w("bp2")[0:1, :], ALU.add).then_inc(done, 1)
                read(dve, L, m, "R", 0)
                chain(dve.tensor_reduce(small, lg, AX.X, ALU.max, negate=True))
                dve.tensor_scalar(total, small, 1.0, None, ALU.mult).then_inc(L.choice_in, 1)

            def choose_out(m):
                lg, top, small, total = choice_views()
                chain = Chain(dve, L.choice, 5, m)
                chain.i = 1
                dve.wait_ge(L.choice_exp, m + 1)
                chain(dve.tensor_reduce(total, lg, AX.X, ALU.add))
                chain(dve.reciprocal(total, total))
                chain(dve.tensor_scalar(lg, lg, total, None, ALU.mult), consts_loaded)
                chain(dve.max(top, lg), consts_loaded)
                need(dve, L.chosen, m)
                dve.max_index(B.sel_i[0:1, :], top, lg).then_inc(L.choice_ready, 1)

            def expert_output(n, p):
                tile, done = full(dve, L, n, "F", 1)
                dve.wait_ge(L.chosen, n + 1)
                dve.tensor_scalar(B.rT[:, :], tile[:, 0:S], B.wsel[:, p, 514:515], 0.3, ALU.add, ALU.mult).then_inc(done, 1)

            def finish(n, p, base):
                dve.wait_ge(L.y_full, n + 1)
                need(dve, L.x_stored, DMA * (n - 1))
                dve.tensor_tensor(B.xo[:, p, :], B.pY[:, 0:S], base, ALU.add).then_inc(L.residual_done, 1)

            def step_0(n, p):
                q = 1 - p
                own, ahead, further = works(n, 0), works(n, 1), works(n, 2)
                gate = lambda b: lambda e: B.gl[:, b, e:e + 1]
                if own:
                    token_mix(n, p, 0)
                    token_mix(n, p, 1)
                if ahead:
                    token_scores(n + 1, 0)
                if own:
                    x1(n, p)
                if further:
                    ln_stats(n + 2, p)
                if ahead:
                    token_scores(n + 1, 1)
                    token_softmax_in(n + 1)
                if own:
                    gate_in(n)
                if ahead:
                    token_softmax_out(n + 1)
                if own:
                    gate_out(n)
                if further:
                    ln_apply(n + 2, p)
                if own:
                    normalise(n)
                    dve.wait_ge(L.xx_ready, n + 1)
                    sum_experts(n, 0, 4, gate(0), B.xx[:, 0:D])
                if ahead:
                    maxima(n + 1, 0, 1)
                if own:
                    sum_experts(n, 1, 4, gate(1), B.xx[:, D:2 * D])
                if ahead:
                    maxima(n + 1, 2, 3)
                if further:
                    remainder(n + 2, p)
                if ahead:
                    maxima(n + 1, 4, 5, 6, 7)
                    split_max(n + 1)
                if further:
                    token_qkv(n + 2, p)
                    values_in(n + 2, p)
                if own:
                    finish(n, p, combine(n, 4, B.xx[:, :]))

            def step_1(n, p):
                own, ahead, further = works(n, 0), works(n, 1), works(n, 2)
                if own:
                    hidden(n, HID1, 0, 1)
                if further:
                    ln_stats(n + 2, p)
                    ln_apply(n + 2, p)
                if ahead:
                    maxima(n + 1, 0, 1, 2)
                if own:
                    normalise(n)
                if ahead:
                    maxima(n + 1, 3)
                if further:
                    rotate(n + 2, p)
                if ahead:
                    maxima(n + 1, 4, 5)
                    split_max(n + 1)
                if further:
                    remainder(n + 2, p)
                    values_in(n + 2, p)
                if own:
                    dve.wait_ge(L.xb_ready, n + 1)
                    finish(n, p, B.xb[:, p, :])

            def step_2(n, p):
                q = 1 - p
                own, ahead, further = works(n, 0), works(n, 1), works(n, 2)
                weight = lambda b: lambda e: B.comb[:, p, b, e:e + 1]
                if ahead:
                    route_in(n + 1)
                if own:
                    hidden(n, CH2, 0, 1, 2, 3, 4, 5, 6, 7)
                if further:
                    ln_stats(n + 2, p)
                    ln_apply(n + 2, p)
                if ahead:
                    route(n + 1, q)
                    maxima(n + 1, 0, 1, 2, 3, 4, 5, 6)
                if own:
                    normalise(n)
                if ahead:
                    maxima(n + 1, 7)
                    split_max(n + 1)
                if own:
                    dve.wait_ge(L.xb_ready, n + 1)
                    sum_experts(n, 0, 8, weight(0), B.xb[:, p, 0:D])
                if further:
                    rotate(n + 2, p)
                    remainder(n + 2, p)
                if own:
                    sum_experts(n, 1, 8, weight(1), B.xb[:, p, D:2 * D])
                if further:
                    values_in(n + 2, p)
                if own:
                    finish(n, p, combine(n, 8, B.xb[:, p, :]))

            def step_3(n, p):
                own, ahead, further = works(n, 0), works(n, 1), works(n, 2)
                if further:
                    ln_stats(n + 2, p)
                if ahead:
                    choose_in(n + 1)
                if own:
                    expert_output(n, p)
                if ahead:
                    choose_out(n + 1)
                if further:
                    ln_apply(n + 2, p)
                if ahead:
                    maxima(n + 1, 0, 1, 2)
                if own:
                    normalise(n)
                if ahead:
                    maxima(n + 1, 3)
                if further:
                    rotate(n + 2, p)
                if ahead:
                    maxima(n + 1, 4, 5)
                    split_max(n + 1)
                if further:
                    remainder(n + 2, p)
                    values_in(n + 2, p)
                if own:
                    dve.wait_ge(L.xb_ready, n + 1)
                    finish(n, p, B.xb[:, p, :])

            prepare()
            steps(dve, [step_0, step_1, step_2, step_3][l])


def gpsimd_program(nc, block, B, layer_state, read, c, consts_loaded, cleared, w_loaded):
    @block.gpsimd
    def _(pool):
        pool.memset(B.V[:, :, :, :], 0.0).then_inc(cleared, 1)
        for i in range(2):
            pool.wait_ge(cleared, 2 * i + 1)
            pool.memset(B.KS[i][64:128, :, :], 1.0).then_inc(cleared, 1)
            pool.wait_ge(cleared, 2 * i + 2)
            pool.memset(B.QS[i][64:128, :, :], 0.0).then_inc(cleared, 1)
        pool.wait_ge(cleared, 5)
        pool.wait_ge(consts_loaded, 2 * DMA)
        for L in layer_state:
            l, w = L.l, L.w
            power = c("neghalf")[:, 0:BLK]

            def rstd(m):
                stats_count, rstd_count = worked_out(pool, 2 * m + 2, m)
                pool.wait_ge(consts_loaded, 2 * DMA)
                pool.wait_ge(L.ln_stats, stats_count)
                need(pool, L.rstd_ready, rstd_count)
                pool.tensor_scalar(B.ve[:, :], B.mv[:, :, 1], 1e-5, None, ALU.add).then_inc(L.ln_var, 1)
                pool.wait_ge(L.ln_var, m + 1)
                need(pool, L.xn_ready, m)
                pool.tensor_tensor(B.rstd[:, :], B.ve[:, :], power, ALU.pow).then_inc(L.rstd_ready, 1)

            def inverse_rms(m, sums, mean, out, ready_in, between, ready_out):
                in_count, out_count = worked_out(pool, m + 1, m)
                pool.wait_ge(consts_loaded, 2 * DMA)
                pool.wait_ge(ready_in, in_count)
                need(pool, ready_out, out_count)
                pool.tensor_scalar(mean, sums, 1.0 / D, 1e-6, ALU.mult, ALU.add).then_inc(between, 1)
                pool.wait_ge(between, m + 1)
                pool.tensor_tensor(out, mean, power, ALU.pow).then_inc(ready_out, 1)

            def base(m, p):
                pool.wait_ge(L.xn_ready, m + 1)
                need(pool, L.residual_done, m - 1)
                t = pool.tensor_tensor(B.xb[:, p, :], B.x[:, p, :], w("bo"), ALU.add)
                if l == 0:
                    t = pool.tensor_tensor(B.x1b[:, p, :], B.xn[:, p, :], w("bo2"), ALU.add)
                if l == 3:
                    t.then_inc(L.pool_sum, 1)
                    pool.wait_ge(L.pool_sum, m + 1)
                    t = pool.tensor_tensor(B.xb[:, p, :], B.xb[:, p, :], B.xn[:, p, :], ALU.add)
                t.then_inc(L.xb_ready, 1)

            def lowest(m, q):
                pool.wait_ge(L.mid_ready, m + 1)
                pool.tensor_tensor(B.parts[:, q, :, 2, :], B.res[:, :, :], B.parts[:, q, :, 1, :], ALU.subtract)\
                    .then_inc(L.parts_ready, 1)

            def score_products(m, q, *bs):
                read(pool, L, m, "A", 3)
                for b in bs:
                    need(pool, L.prod_read, 4 * m + (b - 1))
                    qh = B.tok[:, q, b, 0:D].rearrange("p (h d) -> p h d", d=HD).unsqueeze(2).to_broadcast([P, H, H, HD])
                    kg = B.tok[:, q, b, D:2 * D].rearrange("p (g d) -> p g d", d=HD).unsqueeze(1).to_broadcast([P, H, H, HD])
                    pool.tensor_tensor(B.prod[b].rearrange("p (h g d) -> p h g d", h=H, g=H), qh, kg, ALU.mult)\
                        .then_inc(L.prod_ready, 1)

            def value_products(m, q):
                pool.wait_ge(L.att_ready, m + 1)
                for b in range(BLK):
                    ah = B.att[:, b, :].rearrange("p (h g) -> p h g", h=H).unsqueeze(2).to_broadcast([P, H, HD, H])
                    vd = B.tok[:, q, b, 2 * D:3 * D].rearrange("p (d g) -> p d g", d=HD).unsqueeze(1)\
                        .to_broadcast([P, H, HD, H])
                    pool.tensor_tensor(B.prod[b].rearrange("p (h d g) -> p h d g", h=H, d=HD), ah, vd, ALU.mult)\
                        .then_inc(L.prod_ready, 1)

            def stage_f0(n, p):
                inverse_rms(n, B.ss2[:, :], B.sv[:, 0, :], B.r2[:, :], L.sq2_ready, L.sv2_ready, L.r2_ready)
                read(pool, L, n, "F", 1)
                pool.tensor_tensor(B.xx[:, :], B.x1[:, :], B.xb[:, p, :], ALU.add).then_inc(L.xx_ready, 1)

            def choose(m, q):
                (choice_count,) = worked_out(pool, m + 1)
                pool.wait_ge(consts_loaded, 2 * DMA)
                pool.wait_ge(L.choice_ready, choice_count)
                e = pool.value_load(B.sel_i[0:1, 0:1], min_val=0, max_val=E8 - 1)
                need(pool, L.y_full, m - 1)
                pool.tensor_copy(B.wsel[:, q, :], w("experts")[:, bass.ds(e * EXP3, EXP3)]).then_inc(L.chosen, 1)

            def step(n, p):
                own, ahead, further = works(n, 0), works(n, 1), works(n, 2)
                if l == 0:
                    if ahead:
                        score_products(n + 1, 1 - p, 0, 1)
                    if own:
                        stage_f0(n, p)
                if further:
                    rstd(n + 2)
                if l == 0:
                    if ahead:
                        value_products(n + 1, 1 - p)
                    if further:
                        inverse_rms(n + 2, B.ss[:, p, :], B.sv[:, 1, :], B.r1[:, p, :], L.sq_ready, L.sv_ready, L.r_ready)
                if ahead and l == 3:
                    choose(n + 1, 1 - p)
                if further:
                    lowest(n + 2, p)
                    base(n + 2, p)

            pool.wait_ge(L.prepared, 2 if l == 0 else 1)
            steps(pool, step)


ROUTE = 11


def rope_tables():
    t = np.arange(S, dtype=np.float32)
    inv8 = (np.float32(1.0) / np.float32(10000.0) ** (np.arange(0, HD, 2, dtype=np.float32) / np.float32(HD)))
    f8 = t[:, None] * inv8[None, :].astype(np.float32)
    mixed = np.concatenate([np.sin(f8), np.cos(f8)], axis=-1)
    inv2 = (np.float32(1.0) / np.float32(500.0) ** (np.arange(4, dtype=np.float32) / np.float32(4)))
    f2 = t[:, None] * inv2[None, :].astype(np.float32)
    out = {1: (mixed[:, 1::2], mixed[:, 0::2]), 2: (np.cos(f2), np.sin(f2)), 3: (np.cos(f8), np.sin(f8))}
    rows = {}
    for l, (cos, sin) in out.items():
        cos8 = np.concatenate([cos, cos], axis=1).T
        sin8 = np.concatenate([-sin, sin], axis=1).T
        rows[l] = (np.repeat(cos8, H, axis=0).astype(np.float32), np.repeat(sin8, H, axis=0).astype(np.float32))
    return rows


ROTATE = {1: ([0, 2, 4, 6, 1, 3, 5, 7], [1, 3, 5, 7, 0, 2, 4, 6]), 2: (list(range(8)), [4, 5, 6, 7, 0, 1, 2, 3]),
          3: (list(range(8)), [4, 5, 6, 7, 0, 1, 2, 3])}


def constants():
    const = np.zeros((P, CONST_N), np.float32)
    const[:, :P] = np.eye(P)
    a = CONST["ones"][0]
    for j in range(4):
        const[:, a + 32 * j + HD * j:a + 32 * j + HD * j + HD] = 1.0
    const[:, CONST["iota"][0]:CONST["iota"][1]] = np.arange(E8)
    const[:, CONST["neghalf"][0]:CONST["neghalf"][1]] = -0.5
    above = np.where(np.arange(P)[None, :] > np.arange(P)[:, None], MASKED, 0.0)
    constb = np.concatenate([np.eye(P), above, above, above.T, above.T], axis=1).astype(np.float32)
    return const, constb


def layouts(a):
    f = lambda x: np.asarray(x)
    table = rope_tables()

    def rows(x):
        return np.broadcast_to(f(x)[None, :], (P, f(x).shape[0]))

    def by_dim(wm, dims):
        return np.stack([wm.reshape(wm.shape[0], H, HD)[:, :, d] for d in dims], axis=1).reshape(wm.shape[0], H * HD)

    def padded(wm, n):
        out = np.zeros((n,) + wm.shape[1:], wm.dtype)
        out[:wm.shape[0]] = wm
        return out

    def column(v):
        return f(v).reshape(P, 1)

    packs = []
    def heads8(wm):
        out = np.zeros((P, H, HD), np.float32)
        out[:wm.shape[0], :, :4] = wm.reshape(wm.shape[0], H, 4)
        return out.reshape(P, H * HD)
    Wq, Wk, Wv = (heads8(f(a["L0_attn_" + n]).T) for n in ("Wq", "Wk", "Wv"))
    Wo = np.zeros((H, HD, D), np.float32)
    Wo[:, :4] = f(a["L0_attn_Wo"]).T.reshape(H, 4, D)
    up = f(a["L0_ffn_Wup"]).reshape(64, H, 2, HD)
    bup = f(a["L0_ffn_bup"]).reshape(H, 2, HD)
    kv = lambda x: np.concatenate([x[..., :, 0, :].reshape(x.shape[:-3] + (D,)),
                                   np.swapaxes(x[..., :, 1, :], -1, -2).reshape(x.shape[:-3] + (D,))], axis=-1)
    bdown = np.zeros((P, P), np.float32)
    bdown[:64] = f(a["L0_ffn_bdown"])[:, None]
    zeros = lambda n: np.zeros((P, n), np.float32)
    packs.append(dict(
        q1=by_dim(Wq, range(HD)), k1=by_dim(Wk, range(HD)), v=Wv, bv=zeros(BLK * D), o=Wo.reshape(P, D),
        bo=np.tile(rows(a["L0_attn_bo"]), (1, BLK)), qkv2=np.concatenate([f(a["L0_ffn_Wq"]), zeros(2 * D)], axis=1),
        down=padded(f(a["L0_ffn_Wdown"]).T, P), up=padded(kv(up), P), bdown=bdown, bup=rows(kv(bup)),
        bqkv2=np.concatenate([rows(a["L0_ffn_bq"]), zeros(2 * D)], axis=1), g1=column(a["L0_ffn_gamma1"]),
        g2=column(a["L0_ffn_gamma2"]), o2=f(a["L0_ffn_Wo"]), bo2=np.tile(rows(a["L0_ffn_bo"]), (1, BLK)),
        gate=f(a["L0_ffn_Wg"]), bgate=rows(a["L0_ffn_bg"]),
        experts=f(a["L0_ffn_We"]).transpose(1, 0, 2).reshape(D, E8 * D)))

    def attention(l, wq, wk, wv, bq, bk, bv, wo, bo):
        d1, d2 = ROTATE[l]
        cos, sin = table[l]
        return dict(q1=by_dim(wq, d1), q2=by_dim(wq, d2), k1=by_dim(wk, d1), k2=by_dim(wk, d2), cos=cos, sin=sin,
                    bq1=by_dim(bq[None], d1).reshape(P, 1), bq2=by_dim(bq[None], d2).reshape(P, 1),
                    bk1=by_dim(bk[None], d1).reshape(P, 1), bk2=by_dim(bk[None], d2).reshape(P, 1),
                    v=wv, bv=np.tile(rows(bv), (1, BLK)), o=wo, bo=np.tile(rows(bo), (1, BLK)))

    w, b = f(a["L1_attn_qkv_w"]), f(a["L1_attn_qkv_b"])
    packs.append(attention(1, w[:, :D], w[:, D:2 * D], w[:, 2 * D:], b[:D], b[D:2 * D], b[2 * D:],
                           f(a["L1_attn_out_w"]), a["L1_attn_out_b"]))
    ints = np.concatenate([f(a["L1_ffn_w_gate"]).T, f(a["L1_ffn_w_up"]).T] +
                          [f(a["L1_ffn_w_down"]).T[i * P:(i + 1) * P] for i in range(HID1)], axis=1)

    w, b = f(a["L2_attn_w_qkv"]), f(a["L2_attn_b_qkv"])
    pack = attention(2, w[:, :D], w[:, D:2 * D], w[:, 2 * D:], b[:D], b[D:2 * D], b[2 * D:],
                     f(a["L2_attn_w_out"]), a["L2_attn_b_out"])

    def chunks(experts, shared):
        out = np.zeros((P, CH2, P), np.float32)
        for e in range(E8):
            out[:, e] = experts[e][:, :P]
            out[:, E8 + e // 2, 64 * (e % 2):64 * (e % 2) + 48] = experts[e][:, P:]
        for s in range(3):
            part = shared[:, s * P:(s + 1) * P]
            out[:, 12 + s, :part.shape[1]] = part
        return out.reshape(P, CH2 * P)
    down, shared = f(a["L2_ffn_w_down"]), f(a["L2_ffn_sw_down"])
    rest = np.zeros((P, E8, D), np.float32)
    for e in range(E8):
        rest[64 * (e % 2):64 * (e % 2) + 48, e] = down[e][P:]
    pack.update(
        router=f(a["L2_ffn_gate_w"]).T, gate=chunks(f(a["L2_ffn_w_gate"]), f(a["L2_ffn_sw_gate"])),
        up=chunks(f(a["L2_ffn_w_up"]), f(a["L2_ffn_sw_up"])), down=down[:, :P].transpose(1, 0, 2).reshape(P, E8 * D),
        downr=rest.reshape(P, E8 * D), shared=padded(shared, 3 * P).reshape(3, P, D).transpose(1, 0, 2).reshape(P, 3 * D))
    packs.append(pack)

    nothing = np.zeros(D, np.float32)
    pack = attention(3, f(a["L3_attn_Wq"]).T, f(a["L3_attn_Wk"]).T, f(a["L3_attn_Wv"]).T, nothing, nothing, nothing,
                     f(a["L3_attn_Wo"]).T, a["L3_ffn_bo"])
    w1, b1, w2, b2 = (f(a["L3_ffn_" + n]) for n in ("W1", "b1", "W2", "b2"))
    pack.update(
        p1=f(a["L3_ffn_Wp1"]), bp1=column(a["L3_ffn_bp1"]), p2=f(a["L3_ffn_Wp2"]), bp2=rows(a["L3_ffn_bp2"]),
        experts=np.concatenate([np.concatenate([w1[e], w2[e][:P], w2[e][P:], b1[e].reshape(2, P).T, b2[e].reshape(P, 1)],
                                               axis=1) for e in range(E8)], axis=1), o3=f(a["L3_ffn_Wo"]))
    packs.append(pack)
    laid = []
    for (fields, n), pack in zip(WEIGHTS, packs):
        out = np.zeros((P, n), np.float32)
        for name, (i, j) in fields.items():
            if name != "ffn":
                out[:, i:j] = pack[name]
        laid.append(out)
    return laid, np.ascontiguousarray(ints)


def program(nc, arrays, layers=LAYERS):
    aps = {}
    for name, v in arrays.items():
        aps[name.removesuffix("_dram")] = nc.dram_tensor(name, v.shape, mybir.dt.from_np(v.dtype), kind="ExternalInput").ap()
    out = nc.dram_tensor("out_dram", (NB * S, D), F32, kind="ExternalOutput").ap()
    build(nc, aps["x"], [aps[f"w{l}"] for l in range(4)], aps["ints"], aps["const"], aps["constb"], out, layers)


def arrange(inputs):
    laid, ints = layouts(inputs)
    const, constb = constants()
    arrays = {"x": np.ascontiguousarray(np.asarray(inputs["L0_attn_x"]).reshape(NB * S, D)), "ints": ints,
              "const": const, "constb": constb}
    for l, w in enumerate(laid):
        arrays[f"w{l}"] = w
    return {f"{name}_dram": v for name, v in arrays.items()}


def kernel(**inputs):
    import concourse.bacc as bacc
    from concourse.bass_utils import run_bass_kernel_spmd
    arrays = arrange(inputs)
    nc = bacc.Bacc("TRN2", target_bir_lowering=False, num_devices=1)
    program(nc, arrays)
    r = run_bass_kernel_spmd(nc, [arrays], core_ids=[0])
    return r.results[0]["out_dram"].reshape(NB, S, D)
```

```python
from contextlib import ExitStack

import numpy as np

import concourse.bass as bass
from concourse import mybir

F32 = mybir.dt.float32
BF16 = mybir.dt.bfloat16
I32 = mybir.dt.int32
U32 = mybir.dt.uint32
ALU = mybir.AluOpType
ACT = mybir.ActivationFunctionType
AX = mybir.AxisListType

NB, S, D = 32, 256, 128
P = 128
BLK = S // P
H, HD = 16, 8
PARTS = 3
SLOTS = PARTS * PARTS
ROW_MAX = P - 2
KM, KE = ROW_MAX, P
RING = 3
TILE = 1024
BANK = 512
SCALE = float(1.0 / np.sqrt(np.float32(HD)))
E8 = 8
MASKED = -1e30
LAYERS = 4
DMA = 16


def columns(fields):
    at, out = 0, {}
    for name, n in fields:
        out[name] = (at, at + n)
        at += n
    return out, at


CONST, CONST_N = columns([("ident", P), ("ones", 4 * 32), ("iota", E8), ("neghalf", 4)])
CONSTB, CONSTB_N = columns([("ident", P), ("maskM", 2 * P), ("maskE", 2 * P)])
ROPE_W = [("q1", D), ("q2", D), ("k1", D), ("k2", D), ("cos", S), ("sin", S), ("bq1", 1), ("bq2", 1),
          ("bk1", 1), ("bk2", 1)]
ATTN_W = [("v", D), ("bv", BLK * D), ("o", D), ("bo", BLK * D)]
L0_W = [("q1", D), ("k1", D)] + ATTN_W + [
    ("qkv2", 3 * D), ("down", D), ("up", 2 * D), ("bdown", D), ("bup", 2 * D), ("bqkv2", 3 * D), ("g1", 1), ("g2", 1),
    ("o2", D), ("bo2", BLK * D), ("gate", E8), ("bgate", E8), ("experts", E8 * D)]
HID1 = 384 // P
L1_W = ROPE_W + ATTN_W + [("ffn", 3 * HID1 * P)]
CH2 = 15
L2_W = ROPE_W + ATTN_W + [("router", E8), ("gate", CH2 * P), ("up", CH2 * P), ("down", E8 * D), ("downr", E8 * D),
                          ("shared", 3 * D)]
EXP3 = 256 + 256 + 2 + 1
L3_W = ROPE_W + ATTN_W + [("p1", P), ("bp1", 1), ("p2", E8), ("bp2", E8), ("experts", E8 * EXP3), ("o3", D)]
WEIGHTS = [columns(w) for w in (L0_W, L1_W, L2_W, L3_W)]
CAUSAL = [False, True, False, True]

ORDER = [
    "E0 E1 F0 E2 F1 E3 F2 E4 F3 E5 E6 M0 E7 F4 V F5 M1 A0 M2 M3 M4 A1 A3 M5 M6 M7 Y T0 A2",
    "E0 F1 F0 E1 A0 E2 M0 A1 E3 M1 M2 E4 M3 M4 E5 V A2 M5 T0 Y",
    "F0 F2 F1 F3 F4 F5 F6 F7 E0 E1 A0 M0 E2 M1 A1 E3 M2 E4 M3 E5 M4 E6 M5 E7 M6 V M7 F8 T0 F9 A2 Y",
    "F0 E0 F1 E1 R0 A0 E2 A1 E3 E4 M0 M1 M2 E5 M3 M4 V M5 Y A2 T0",
]
AHEAD = {"A": 2, "M": 1, "R": 1, "T": 1, "E": 0, "F": 0, "V": 0, "Y": 0}

SCALAR_ORDER = [
    "E0 E1 load F0 E2 E3 F2 E4 E5 tokens router E6 E7 F4 F5 A0 high middle T0",
    "E0 F0 F1 E1 load A0 E2 E3 high E4 E5 middle T0",
    "F0 router F1 F2 load F3 F4 F5 F6 F7 E0 E1 A0 E2 E3 high E4 E5 middle E6 E7 T0",
    "F0 hidden E0 E1 load A0 choice E2 E3 high E4 E5 middle T0",
]
VECTOR_ORDER = [
    "mix1 scores0 F1 scores1 softmax_in F3 softmax_out stats gate M0 V M1 norm M2 M3 mix0 M4 rest A3 M5 M6 M7 "
    "split A2 finish",
    "F0 F1 M0 stats A1 M1 M2 norm rest M3 M4 V M5 split A2 finish",
    "F0 route_in F2 F1 F3 F4 F5 F6 stats F7 route M0 M1 A1 norm M2 rest M3 M4 M5 M6 M7 split V F8 A2 F9 finish",
    "F1 R0 chosen A1 stats rest norm M0 M1 M2 M3 M4 V M5 split A2 finish",
]
GPSIMD_ORDER = [
    "products1 x1 rstd values lowest inverse_rms products0 base",
    "rstd lowest base",
    "rstd lowest base",
    "choose rstd lowest base",
]


class Names:
    pass


def need(engine, sem, count):
    if isinstance(count, int) and count <= 0:
        return
    engine.wait_ge(sem, count)


def worked_out(engine, *counts):
    return [n if isinstance(n, int) else engine.to_reg(n) for n in counts]


def works(n, batches_ahead):
    return not isinstance(n, int) or 0 <= n + batches_ahead < NB


def in_order(order, actions):
    def step(n, p):
        for word in order.split():
            ahead, action = actions[word]
            if works(n, ahead):
                action(n + ahead, (p + ahead) % 2)
    return step


def steps(engine, step):
    for n in range(-3, 4):
        step(n, n % 2)
    with engine.Fori(2, NB // 2 - 2) as pair:
        step(pair * 2, 0)
        step(pair * 2 + 1, 1)
    for n in range(NB - 4, NB):
        step(n, n % 2)


class Ring:

    def __init__(self, order):
        tiles = [(piece[0], int(piece[1:])) for piece in order.split() if len(piece) > 1]
        self.lay(tiles, 0)
        self.per_step = self.held
        self.steps = {}
        start = [0] * RING
        for n in range(-3, NB):
            places = self.lay([t for t in tiles if works(n, AHEAD[t[0]])], start)
            self.steps[n] = places
            start = self.held

    def lay(self, tiles, start):
        held, places = list(start or [0] * RING), {}
        for at, tile in enumerate(tiles):
            s = at % RING
            places[tile] = (s, held[s])
            held[s] += 1
        self.held = held
        return places

    def at(self, m, name, k):
        if isinstance(m, int):
            return self.steps[m - AHEAD[name]][name, k]
        slot, before = self.steps[0][name, k]
        return slot, (m - AHEAD[name]) * self.per_step[slot] + before


def build(nc, x_in_dram, weights_dram, ints_dram, const_dram, constb_dram, out_dram, layers=LAYERS):
    with ExitStack() as ctx:
        def sb(name, shape, dt=F32):
            return ctx.enter_context(nc.sbuf_tensor(name, shape, dt))

        def psum(name, shape):
            return ctx.enter_context(nc.psum_tensor(name, shape, F32))

        def sem(name):
            return ctx.enter_context(nc.semaphore(name))

        ring = [psum(f"ring{i}", [P, TILE]) for i in range(RING)]
        pOZ = psum("pOZ", [P, BANK])
        pY = psum("pY", [P, BANK])

        const = sb("const_sb", [P, CONST_N])
        constb = sb("constb_sb", [P, CONSTB_N], BF16)
        even = max(WEIGHTS[0][1], WEIGHTS[2][1])
        odd = max(WEIGHTS[1][1], WEIGHTS[3][1])
        w_sb = [sb("w_even", [P, even]), sb("w_odd", [P, odd])]
        xres = sb("xres", [P, NB, S])
        B = Names()
        B.ring = ring
        B.pOZ = pOZ
        B.pY = pY
        B.x = sb("x", [P, 2, S])
        B.stats = sb("stats", [P, BLK, 6])
        B.mv = sb("mv", [P, BLK, 2])
        B.ve = sb("ve", [P, BLK])
        B.rstd = sb("rstd", [P, BLK])
        B.xn = sb("xn", [P, 2, S])
        B.xb = sb("xb", [P, 2, S])
        B.xnT = sb("xnT", [P, 2, S])
        B.rt = sb("rt", [P, 4, S])
        B.qk = sb("qk", [P, 2, S])
        B.res = sb("res", [P, 2, S])
        B.parts = sb("parts", [P, 2, 2, PARTS, S], BF16)
        B.QS = [sb(f"QS{i}", [P, H, S], BF16) for i in range(2)]
        B.KS = [sb(f"KS{i}", [P, H, S], BF16) for i in range(2)]
        B.V = sb("V", [P, 2, BLK, H * 32])
        B.prob = sb("prob", [P, 2, TILE])
        B.nm = sb("nm", [P, BLK, H])
        B.nms = sb("nms", [P, BLK, 2, H], BF16)
        B.nmT = sb("nmT", [32, 2, S], BF16)
        B.rz = sb("rz", [P, S])
        B.on = sb("on", [P, S])
        B.xo = sb("xo", [P, 2, S])
        B.acc = sb("acc", [P, BLK, D])
        B.g = sb("g", [P, CH2, S])
        B.sg = sb("sg", [P, 2, BANK])
        B.tok = sb("tok", [P, 2, BLK, 3 * D])
        B.prod1 = sb("prod1", [P, H * H * HD])
        B.am = sb("am", [P, BLK, H])
        B.mix = sb("mix", [P, 2, S])
        B.ss = sb("ss", [P, 2, BLK])
        B.sv = sb("sv", [P, 2, BLK])
        B.r1 = sb("r1", [P, 2, BLK])
        B.r2 = sb("r2", [P, BLK])
        B.ss2 = sb("ss2", [P, BLK])
        B.gl = sb("gl", [P, BLK, E8])
        B.gs = sb("gs", [P, BLK])
        B.comb = sb("comb", [P, 2, BLK, E8])
        B.top = sb("top", [P, BLK, E8])
        B.idx = sb("idx", [P, BLK, E8], U32)
        B.idxf = sb("idxf", [P, BLK, 2])
        B.wt = sb("wt", [P, BLK, 2])
        B.one = sb("one", [P, BLK, E8])
        B.sel_h = sb("sel_h", [P, 1])
        B.sel_g = sb("sel_g", [P, 1])
        B.sel = sb("sel", [1, 4 * E8])
        B.sel_i = sb("sel_i", [1, E8], U32)
        B.wsel = sb("wsel", [P, 2, EXP3])
        B.sq, B.mixT, B.x1T, B.xx = B.sg[:, 0, 0:S], B.sg[:, 0, S:2 * S], B.sg[:, 1, 0:S], B.sg[:, 1, S:2 * S]
        B.x1b, B.x1, B.att, B.rT = B.rt[:, 0:2, :], B.rt[:, 2, :], B.qk, B.sg[:, 0, 0:S]
        B.weighted = [B.g[:, 8:12, :].rearrange("p a t -> p (a t)"),
                      B.wsel[:, :, :].rearrange("p a t -> p (a t)")[:, 0:E8 * D]]
        B.prod = [B.g[:, 0:8, :].rearrange("p a t -> p (a t)"), B.prod1[:, :]]
        c = lambda name: const[:, CONST[name][0]:CONST[name][1]]
        cb = lambda name: constb[:, CONSTB[name][0]:CONSTB[name][1]]
        ident, identb = c("ident"), cb("ident")
        B.staged = B.g[:, 0:3, :].rearrange("p a t -> p (a t)")[:, 0:CONSTB_N]

        consts_loaded = sem("consts_loaded")
        cleared = sem("cleared")
        constb_ready = sem("constb_ready")
        w_loaded = [sem(f"w_loaded{i}") for i in range(layers)]

        block = ctx.enter_context(nc.Block())
        layer_state = []
        for l in range(layers):
            q = f"L{l}_"
            TE = 6 if CAUSAL[l] else 8
            L = Names()
            L.l = l
            L.causal = CAUSAL[l]
            L.rope = l > 0
            L.TE = TE
            L.tile_full = [sem(f"{q}tile_full{i}") for i in range(RING)]
            L.tile_read = [sem(f"{q}tile_read{i}") for i in range(RING)]
            L.x_loaded = sem(q + "x_loaded")
            L.ln_stats = sem(q + "ln_stats")
            L.ln_var = sem(q + "ln_var")
            L.rstd_ready = sem(q + "rstd_ready")
            L.xn_ready = sem(q + "xn_ready")
            L.xb_ready = sem(q + "xb_ready")
            L.hi_ready = sem(q + "hi_ready")
            L.mid_ready = sem(q + "mid_ready")
            L.parts_ready = sem(q + "parts_ready")
            L.stacked = sem(q + "stacked")
            L.max_split = sem(q + "max_split")
            L.max_placed = sem(q + "max_placed")
            L.pv_done = sem(q + "pv_done")
            L.rz_ready = sem(q + "rz_ready")
            L.on_ready = sem(q + "on_ready")
            L.y_full = sem(q + "y_full")
            L.residual_done = sem(q + "residual_done")
            L.x_stored = sem(q + "x_stored")
            L.prepared = sem(q + "prepared")
            if l > 0:
                L.qk_ready, L.res_ready = sem(q + "qk_ready"), sem(q + "res_ready")
            if l == 3:
                L.pool_sum = sem(q + "pool_sum")
            if l == 2:
                L.experts_summed = sem(q + "experts_summed")
            if l in (0, 2):
                L.router, L.router_exp, L.router_in = sem(q + "router"), sem(q + "router_exp"), sem(q + "router_in")
                L.gate_ready = sem(q + "gate_ready")
            if l == 0:
                L.sq_ready, L.sv_ready, L.r_ready = sem(q + "sq_ready"), sem(q + "sv_ready"), sem(q + "r_ready")
                L.tok_ready, L.prod_ready, L.prod_read = sem(q + "tok_ready"), sem(q + "prod_ready"), sem(q + "prod_read")
                L.token, L.att_in, L.att_exp = sem(q + "token"), sem(q + "att_in"), sem(q + "att_exp")
                L.att_ready, L.xx_ready = sem(q + "att_ready"), sem(q + "xx_ready")
                L.sq2_ready, L.sv2_ready, L.r2_ready = sem(q + "sq2_ready"), sem(q + "sv2_ready"), sem(q + "r2_ready")
            if l in (1, 2):
                L.gated = sem(q + "gated")
            if l == 3:
                L.gelu_ready, L.choice, L.choice_in = sem(q + "gelu_ready"), sem(q + "choice"), sem(q + "choice_in")
                L.choice_exp, L.choice_ready, L.chosen = sem(q + "choice_exp"), sem(q + "choice_ready"), sem(q + "chosen")
                L.r_ready = sem(q + "r_ready")
            L.ring = Ring(ORDER[l])
            fields = WEIGHTS[l][0]
            L.w = (lambda fields, l: lambda name, a=0, b=None: w_sb[l % 2][
                :, fields[name][0] + a:fields[name][0] + b if b is not None else fields[name][1]])(fields, l)
            layer_state.append(L)

        def full(engine, L, m, name, k):
            slot, before = L.ring.at(m, name, k)
            engine.wait_ge(L.tile_full[slot], before + 1)
            return ring[slot], L.tile_read[slot]

        def read(engine, L, m, name, k):
            slot, before = L.ring.at(m, name, k)
            engine.wait_ge(L.tile_read[slot], before + 1)

        dram = Names()
        dram.x, dram.w, dram.ints, dram.out = x_in_dram, weights_dram, ints_dram, out_dram
        dram.const, dram.constb = const_dram, constb_dram
        sync_program(nc, block, B, layer_state, read, dram, const, w_sb, xres, consts_loaded, w_loaded)
        tensor_program(nc, block, B, layer_state, ring, pOZ, pY, c, ident, identb, cb, consts_loaded, cleared, constb_ready, w_loaded, read)
        scalar_program(nc, block, B, layer_state, full, read, dram, xres)
        vector_program(nc, block, B, layer_state, full, read, c, w_loaded, consts_loaded, constb, constb_ready)
        gpsimd_program(nc, block, B, layer_state, read, c, consts_loaded, cleared, w_loaded)


def sync_program(nc, block, B, layer_state, read, dram, const, w_sb, xres, consts_loaded, w_loaded):
    @block.sync
    def _(sp):
        def load_weights(l):
            n = WEIGHTS[l][1]
            if l == 1:
                a, b = WEIGHTS[1][0]["ffn"]
                sp.dma_start(w_sb[1][:, 0:a], dram.w[1][:, 0:a]).then_inc(w_loaded[1], DMA)
                sp.dma_start(w_sb[1][:, a:b].bitcast(I32), dram.ints).then_inc(w_loaded[1], DMA)
            else:
                sp.dma_start(w_sb[l % 2][:, 0:n], dram.w[l]).then_inc(w_loaded[l], DMA)

        sp.dma_start(const[:, :], dram.const).then_inc(consts_loaded, DMA)
        sp.dma_start(B.staged, dram.constb).then_inc(consts_loaded, DMA)
        for L in layer_state:
            l, last = L.l, L.l == len(layer_state) - 1

            if l == 0:
                load_weights(0)
            if l + 1 < len(layer_state):
                load_weights(l + 1)

            def stack(p, part):
                for s in range(SLOTS):
                    rows = slice(HD * s, HD * s + HD)
                    if s // PARTS == part:
                        sp.dma_start(B.QS[p][rows, :, :], B.parts[:, p, 0, part, :]).then_inc(L.stacked, DMA)
                    if s % PARTS == part:
                        sp.dma_start(B.KS[p][rows, :, :], B.parts[:, p, 1, part, :]).then_inc(L.stacked, DMA)

            def step(n, p):
                if works(n, 2):
                    m = n + 2
                    ready_count, pv_count = worked_out(sp, m + 1, (m - 1) * L.TE)
                    need(sp, L.pv_done, pv_count)
                    if isinstance(n, int) and m == 1:
                        read(sp, L, 0, "M", 0)
                    sp.wait_ge(L.hi_ready, ready_count)
                    stack(p, 0)
                if works(n, 1):
                    read(sp, L, n + 1, "T", 0)
                    for part in range(2):
                        sp.dma_start(B.QS[1 - p][ROW_MAX + part:ROW_MAX + part + 1, :, :],
                                     B.nmT[H * part:H * part + H, 1 - p, :]).then_inc(L.max_placed, DMA)
                if works(n, 2):
                    (ready_count,) = worked_out(sp, n + 3)
                    sp.wait_ge(L.mid_ready, ready_count)
                    stack(p, 1)
                    sp.wait_ge(L.parts_ready, ready_count)
                    stack(p, 2)
                if works(n, 0):
                    done_count, stored_count = worked_out(sp, n + 1, DMA * n)
                    sp.wait_ge(L.residual_done, done_count)
                    need(sp, L.x_stored, stored_count)
                    if last:
                        dst = dram.out[bass.ts(n, S), :].rearrange("(b p) d -> p b d", p=P)
                        sp.dma_start(dst, B.xo[:, p, :].rearrange("p (b d) -> p b d", d=D)).then_inc(L.x_stored, DMA)
                    else:
                        sp.dma_start(xres[:, n, :], B.xo[:, p, :]).then_inc(L.x_stored, DMA)

            steps(sp, step)
            sp.wait_ge(L.x_stored, NB * DMA)


def m_tiles(causal):
    if causal:
        return [(0, 8 * t, 8, P) for t in range(2)] + [(1, 4 * t, 4, S) for t in range(4)]
    return [(b, 4 * t, 4, S) for b in range(BLK) for t in range(4)]


def e_tiles(causal):
    group = lambda j: [4 * i + j for i in range(4)]
    if causal:
        return [(0, group(j), 0, S) for j in range(4)] + [(1, group(j) + group(j + 1), P, P) for j in (0, 2)]
    return [(b, group(j), 0, S) for b in range(BLK) for j in range(4)]


def tensor_program(nc, block, B, layer_state, ring, pOZ, pY, c, ident, identb, cb, consts_loaded, cleared, constb_ready, w_loaded, read):
    @block.tensor
    def _(pe):
        pe.wait_ge(consts_loaded, 2 * DMA)
        pe.wait_ge(cleared, 5)
        pe.wait_ge(constb_ready, 1)
        for L in layer_state:
            l = L.l
            w = L.w

            def take(m, name, k):
                slot, before = L.ring.at(m, name, k)
                need(pe, L.tile_read[slot], before)
                return ring[slot], L.tile_full[slot]

            def mm(out, lhsT, rhs, start=True, stop=True, loose=False):
                return pe.matmul(out, lhsT, rhs, start=start, stop=stop, skip_group_check=loose)

            def blocks(T, b):
                return T[:, b * P:(b + 1) * P]

            def stage_a(m, q, k):
                xT = B.xnT[:, q, :]
                if k == 0:
                    pe.wait_ge(L.xn_ready, m + 1)
                if k == 1:
                    read(pe, L, m, "A", 0)
                tile, filled = take(m, "A", k)
                if k == 0:
                    for b in range(BLK):
                        t = pe.transpose(tile[:, b * P:(b + 1) * P], B.xn[:, q, b * P:(b + 1) * P], ident)
                if k == 1:
                    for i, name in enumerate(["q1", "q2", "k1", "k2"] if L.rope else ["q1", "k1"]):
                        t = mm(tile[:, i * S:(i + 1) * S], w(name), xT)
                if k == 2:
                    for b in range(BLK):
                        t = mm(tile[:, b * P:(b + 1) * P], blocks(xT, b), w("v"))
                    if l == 2:
                        for b in range(BLK):
                            t = mm(tile[:, BANK + E8 * b:BANK + E8 * b + E8], blocks(xT, b), w("router"))
                    if l == 3:
                        t = mm(tile[:, BANK:BANK + 1], w("p1"), xT[:, S - 1:S])
                if k == 3:
                    for b in range(BLK):
                        t = mm(tile[:, b * BANK:b * BANK + 3 * D], blocks(xT, b), w("qkv2"))
                t.then_inc(filled, 1)

            def stage_m(m, q, k):
                if k == 0:
                    pe.wait_ge(L.stacked, 2 * SLOTS * DMA * m + 2 * SLOTS * DMA)
                b, h0, heads, keys = m_tiles(L.causal)[k]
                tile, filled = take(m, "M", k)
                per_bank = BANK // keys
                for i in range(heads):
                    at = i * keys
                    if L.causal and i % per_bank == 0:
                        diag = tile[:, at:at + BANK].rearrange("p (h k) -> p h k", k=keys)[:, :, keys - P:keys]
                        for j in range(0, per_bank, 2):
                            mm(diag[:, j:j + 2, :], identb, cb("maskM").rearrange("p (h k) -> p h k", k=P),
                               start=j == 0, stop=False, loose=True)
                    t = mm(tile[:, at:at + keys], B.QS[q][0:KM, h0 + i, b * P:(b + 1) * P],
                           B.KS[q][0:KM, h0 + i, 0:keys], start=not L.causal, stop=True, loose=L.causal)
                t.then_inc(filled, 1)

            def stage_t(m, q, k):
                pe.wait_ge(L.max_split, 2 * m + 2)
                tile, filled = take(m, "T", 0)
                for b in range(BLK):
                    t = pe.transpose(tile[0:32, b * 64:(b + 1) * 64].bitcast(BF16),
                                     B.nms[:, b, :, :].rearrange("p a h -> p (a h)"), identb)
                t.then_inc(filled, 1)

            def stage_e(n, p, k):
                if k == 0:
                    pe.wait_ge(L.max_placed, 2 * DMA * n + 2 * DMA)
                scores(n, p, k)
                if k > 0:
                    values(n, p, k - 1)

            def scores(n, p, k):
                b, heads, q0, queries = e_tiles(L.causal)[k]
                tile, filled = take(n, "E", k)
                per_bank = BANK // queries
                for i, h in enumerate(heads):
                    at = i * queries
                    if L.causal and i % per_bank == 0:
                        diag = tile[:, at:at + BANK].rearrange("p (h k) -> p h k", k=queries)[:, :, 0:P]
                        for j in range(0, per_bank, 2):
                            mm(diag[:, j:j + 2, :], identb, cb("maskE").rearrange("p (h k) -> p h k", k=P),
                               start=j == 0, stop=False, loose=True)
                    t = mm(tile[:, at:at + queries], B.KS[p][0:KE, h, b * P:(b + 1) * P],
                           B.QS[p][0:KE, h, q0:q0 + queries], start=not L.causal, stop=True, loose=L.causal)
                t.then_inc(filled, 1)

            def values(n, p, k):
                if k == 0:
                    need(pe, L.on_ready, n)
                b, heads, q0, queries = e_tiles(L.causal)[k]
                read(pe, L, n, "E", k)
                prob = B.prob[:, k % 2, :]
                for o, col in ((0, "v"), (1, "ones")):
                    for i, h in enumerate(heads):
                        g, j = h // 4, h % 4
                        lhsT = B.V[:, p, b, h * 32:h * 32 + 32] if o == 0 else c("ones")[:, 32 * j:32 * j + 32]
                        t = mm(pOZ[32 * g:32 * g + 32, o * S + q0:o * S + q0 + queries], lhsT,
                               prob[:, i * queries:(i + 1) * queries],
                               start=(k == 0 and o == 0), stop=True, loose=True)
                t.then_inc(L.pv_done, 1)


            def attention_out(n, start=True, stop=False):
                pe.wait_ge(L.on_ready, n + 1)
                need(pe, L.residual_done, n)
                for b in range(BLK):
                    t = mm(pY[:, b * D:(b + 1) * D], blocks(B.on, b), w("o"), start=start and b == 0, stop=stop,
                           loose=True)
                return t

            def stage_f0(n, p, k):
                if k == 0:
                    pe.wait_ge(L.prod_read, 4 * n + 4)
                if k in (1, 2, 3):
                    read(pe, L, n, "F", k - 1)
                tile, filled = take(n, "F", k)
                if k >= 4:
                    for half in range(2):
                        t = mm(tile[:, half * BANK:(half + 1) * BANK], blocks(B.x1T, k - 4),
                               w("experts", half * BANK, (half + 1) * BANK))
                else:
                    for b in range(BLK):
                        if k == 0:
                            t = pe.transpose(tile[:, b * P:(b + 1) * P], B.mix[:, p, b * P:(b + 1) * P], ident)
                        if k == 1:
                            t = mm(tile[:, b * P:(b + 1) * P], blocks(B.mixT, b), w("o2"))
                        if k == 2:
                            t = pe.transpose(tile[:, b * P:(b + 1) * P], B.x1[:, b * P:(b + 1) * P], ident)
                        if k == 3:
                            t = mm(tile[:, b * E8:(b + 1) * E8], blocks(B.x1T, b), w("gate"))
                t.then_inc(filled, 1)

            def up_tile(n, p, k, chunks, gate, up):
                tile, filled = take(n, "F", k)
                for half, name, base in ((0, gate, 0), (1, up[0], up[1])):
                    for ch in range(2 * k, min(2 * k + 2, chunks)):
                        t = mm(tile[:, half * BANK + (ch % 2) * S:half * BANK + (ch % 2) * S + S],
                               w(name, base + ch * P, base + (ch + 1) * P), B.xnT[:, p, :])
                t.then_inc(filled, 1)

            def stage_f1(n, p, k):
                up_tile(n, p, k, HID1, "ffn", ("ffn", HID1 * P))

            def stage_f2(n, p, k):
                if k < 8:
                    up_tile(n, p, k, CH2, "gate", ("up", 0))
                    return
                b = k - 8
                tile, filled = take(n, "F", k)
                for e in range(E8):
                    out = tile[:, e * D:(e + 1) * D]
                    mm(out, blocks(B.g[:, e, :], b), w("down", e * D, (e + 1) * D), stop=False)
                    t = mm(out, blocks(B.g[:, E8 + e // 2, :], b), w("downr", e * D, (e + 1) * D), start=False)
                t.then_inc(filled, 1)

            def stage_r(m, q, k):
                pe.wait_ge(L.gelu_ready, m + 1)
                tile, filled = take(m, "R", 0)
                mm(tile[0:1, 0:E8], B.sel_g[:, 0:1], w("p2")).then_inc(filled, 1)

            def stage_f3(n, p, k):
                if k == 0:
                    pe.wait_ge(L.chosen, n + 1)
                else:
                    read(pe, L, n, "F", 0)
                tile, filled = take(n, "F", k)
                for ch in range(2):
                    if k == 0:
                        t = mm(tile[:, ch * S:(ch + 1) * S], B.wsel[:, p, ch * P:(ch + 1) * P], B.xnT[:, p, :])
                    else:
                        t = mm(tile[:, 0:S], B.wsel[:, p, 256 + ch * P:256 + (ch + 1) * P], B.g[:, ch, :],
                               start=ch == 0, stop=ch == 1)
                t.then_inc(filled, 1)

            def output(n):
                t = attention_out(n)
                if l == 0:
                    for b in range(BLK):
                        read(pe, L, n, "F", 4 + b)
                        for e in range(E8):
                            t = mm(pY[:, b * D:(b + 1) * D], ident, B.weighted[b][:, e * D:(e + 1) * D], start=False,
                                   stop=e == E8 - 1, loose=True)
                if l == 1:
                    for ch in range(HID1):
                        if ch % 2 == 0:
                            read(pe, L, n, "F", ch // 2)
                        for b in range(BLK):
                            t = mm(pY[:, b * D:(b + 1) * D], blocks(B.g[:, ch, :], b),
                                   w("ffn", (2 * HID1 + ch) * P, (2 * HID1 + ch + 1) * P), start=False,
                                   stop=ch == HID1 - 1, loose=True)
                if l == 2:
                    read(pe, L, n, "F", 7)
                    for s in range(3):
                        for b in range(BLK):
                            t = mm(pY[:, b * D:(b + 1) * D], blocks(B.g[:, 12 + s, :], b),
                                   w("shared", s * D, (s + 1) * D), start=False, stop=s == 2, loose=True)
                if l == 3:
                    read(pe, L, n, "F", 1)
                    for b in range(BLK):
                        t = mm(pY[:, b * D:(b + 1) * D], blocks(B.rT, b), w("o3"), start=False, stop=True, loose=True)
                t.then_inc(L.y_full, 1)

            stage_f = [stage_f0, stage_f1, stage_f2, stage_f3][l]

            def step(n, p):
                for piece in ORDER[l].split():
                    name, k = piece[0], int(piece[1:] or 0)
                    if not works(n, AHEAD[name]):
                        continue
                    m, parity = n + AHEAD[name], (p + AHEAD[name]) % 2
                    if name == "V":
                        values(m, parity, L.TE - 1)
                    elif name == "Y":
                        output(m)
                    else:
                        {"A": stage_a, "M": stage_m, "R": stage_r, "T": stage_t, "E": stage_e, "F": stage_f}[name](m, parity, k)

            if l == 0:
                pe.wait_ge(w_loaded[0], DMA)
                mm(ring[0][:, 0:2 * D], w("down"), w("up"))
                mm(ring[0][:, BANK:BANK + 2 * D], w("bdown"), w("up")).then_inc(L.prepared, 1)
            pe.wait_ge(L.prepared, 2 if l == 0 else 1)
            steps(pe, step)


class Chain:

    def __init__(self, engine, sem, per, m):
        self.engine, self.sem, self.per, self.m, self.i = engine, sem, per, m, 0

    def __call__(self, instruction, constants=None):
        self.i += 1
        assert self.i <= self.per
        instruction.then_inc(self.sem, 1)
        (count,) = worked_out(self.engine, self.m * self.per + self.i)
        if constants is not None:
            self.engine.wait_ge(constants, 2 * DMA)
        self.engine.wait_ge(self.sem, count)


def scalar_program(nc, block, B, layer_state, full, read, dram, xres):
    @block.scalar
    def _(act):
        for L in layer_state:
            l = L.l
            if l > 0:
                act.wait_ge(layer_state[l - 1].x_stored, NB * DMA)

            def load(m, p):
                xb_count, loaded_count = worked_out(act, m - 1, DMA * m)
                need(act, L.xb_ready, xb_count)
                need(act, L.x_loaded, loaded_count)
                if l == 0:
                    src = dram.x[bass.ts(m, S), :].rearrange("(b p) d -> p b d", p=P)
                    act.dma_start(B.x[:, p, :].rearrange("p (b d) -> p b d", d=D), src).then_inc(L.x_loaded, DMA)
                else:
                    act.dma_start(B.x[:, p, :], xres[:, m, :]).then_inc(L.x_loaded, DMA)

            def transposed(m, q):
                tile, done = full(act, L, m, "A", 0)
                if l > 0 and not (isinstance(m, int) and m < 2):
                    read(act, L, m - 2, "F", (0, 1, 7, 0)[l])
                act.activation(B.xnT[:, q, :], tile[:, 0:S], ACT.Copy).then_inc(done, 1)

            def high(m, q):
                if L.rope:
                    act.wait_ge(L.qk_ready, m + 1)
                    src = B.qk[:, :, :]
                else:
                    tile, done = full(act, L, m, "A", 1)
                    src = tile[:, 0:2 * S].rearrange("p (a t) -> p a t", a=2)
                need(act, L.stacked, 2 * SLOTS * DMA * (m - 1))
                act.activation(B.parts[:, q, :, 0, :], src, ACT.Copy).then_inc(L.hi_ready, 1)

            def middle(m, q):
                if L.rope:
                    act.wait_ge(L.res_ready, m + 1)
                else:
                    read(act, L, m, "A", 1)
                act.activation(B.parts[:, q, :, 1, :], B.res[:, :, :], ACT.Copy).then_inc(L.mid_ready, 1)

            def exponentials(n, k):
                tile, done = full(act, L, n, "E", k)
                need(act, L.pv_done, L.TE * n + (k - 1))
                act.activation(B.prob[:, k % 2, :], tile[:, :], ACT.Exp, scale=SCALE).then_inc(done, 1)

            def maximum_transposed(m, q):
                tile, done = full(act, L, m, "T", 0)
                need(act, L.max_placed, 2 * DMA * (m - 1))
                act.activation(B.nmT[:, q, :], tile[0:32, 0:P].bitcast(BF16), ACT.Copy).then_inc(done, 1)

            def copy_tile(n, k, dst):
                tile, done = full(act, L, n, "F", k)
                act.activation(dst, tile[:, 0:S], ACT.Copy).then_inc(done, 1)

            def router_exp(m):
                act.wait_ge(L.router_in, m + 1)
                act.activation(B.gl[:, :, :], B.gl[:, :, :], ACT.Exp).then_inc(L.router_exp, 1)

            def gates(n, chunks, k):
                tile, _ = full(act, L, n, "F", k)
                width = S * min(2, chunks - 2 * k)
                if k >= 2:
                    read(act, L, n, "F", k - 2)
                act.activation(B.sg[:, k % 2, 0:width], tile[:, 0:width], ACT.Silu).then_inc(L.gated, 1)

            def token_exp(m, p):
                act.wait_ge(L.att_in, m + 1)
                act.activation(B.att[:, :, :], B.att[:, :, :], ACT.Exp, scale=SCALE).then_inc(L.att_exp, 1)

            def weighted_experts(m, b):
                tile, done = full(act, L, m, "F", 4 + b)
                act.wait_ge(L.gate_ready, m + 1)
                for e in range(E8):
                    t = act.activation(B.weighted[b][:, e * D:(e + 1) * D], tile[:, e * D:(e + 1) * D], ACT.Copy,
                                       scale=B.gl[:, b, e:e + 1])
                t.then_inc(done, 1)

            def expert_hidden(m, p):
                tile, done = full(act, L, m, "F", 0)
                act.wait_ge(L.chosen, m + 1)
                for ch in range(2):
                    t = act.activation(B.g[:, ch, :], tile[:, ch * S:(ch + 1) * S], ACT.Gelu,
                                       bias=B.wsel[:, p, 512 + ch:513 + ch])
                t.then_inc(done, 1)

            def choice_hidden(m, p):
                read(act, L, m, "A", 2)
                act.activation(B.sel_g[:, 0:1], B.sel_h[:, 0:1], ACT.Gelu).then_inc(L.gelu_ready, 1)

            def choice_exp(m, p):
                act.wait_ge(L.choice_in, m + 1)
                act.activation(B.sel[0:1, 0:E8], B.sel[0:1, 0:E8], ACT.Exp, bias=B.sel[0:1, 2 * E8:2 * E8 + 1])\
                   .then_inc(L.choice_exp, 1)

            actions = {
                "load": (3, load), "A0": (2, transposed), "high": (2, high), "middle": (2, middle), "T0": (1, maximum_transposed),
                "tokens": (1, token_exp), "hidden": (1, choice_hidden), "choice": (1, choice_exp),
                "router": (0 if l == 0 else 1, lambda m, p: router_exp(m))}
            for k in range(L.TE):
                actions[f"E{k}"] = (0, lambda m, p, k=k: exponentials(m, k))
            for k in range(8):
                if l == 0 and k < 4:
                    actions[f"F{k}"] = (0, lambda m, p, k=k: copy_tile(m, k, {0: B.mixT[:, :], 2: B.x1T[:, :]}[k]))
                elif l == 0:
                    actions[f"F{k}"] = (0, lambda m, p, k=k: weighted_experts(m, k - 4))
                elif l == 3:
                    actions[f"F{k}"] = (0, expert_hidden)
                else:
                    actions[f"F{k}"] = (0, lambda m, p, k=k: gates(m, (0, HID1, CH2)[l], k))
            steps(act, in_order(SCALAR_ORDER[l], actions))


def vector_program(nc, block, B, layer_state, full, read, c, w_loaded, consts_loaded, constb, constb_ready):
    @block.vector
    def _(dve):
        dve.wait_ge(consts_loaded, 2 * DMA)
        dve.tensor_copy(constb[:, :], B.staged).then_inc(constb_ready, 1)
        for L in layer_state:
            l, w = L.l, L.w

            def prepare():
                dve.wait_ge(w_loaded[l], DMA * (2 if l == 1 else 1))
                if l == 0:
                    g1, g2 = w("g1"), w("g2")
                    dve.tensor_scalar(w("qkv2", 0, D), w("qkv2", 0, D), g1, None, ALU.mult)
                    dve.tensor_scalar(w("gate"), w("gate"), g2, None, ALU.mult)
                    dve.tensor_scalar(w("experts"), w("experts"), g2, None, ALU.mult)
                    dve.wait_ge(L.prepared, 1)
                    dve.tensor_scalar(w("qkv2", D, 3 * D), B.ring[0][:, 0:2 * D], g1, None, ALU.mult)
                    t = dve.tensor_tensor(w("bqkv2", D, 3 * D), B.ring[0][:, BANK:BANK + 2 * D], w("bup"), ALU.add)
                elif l == 1:
                    t = dve.tensor_scalar(w("ffn"), w("ffn").bitcast(I32), float(np.float32(1.0 / 127.0)), None, ALU.mult)
                elif l == 2:
                    t = dve.tensor_scalar(w("bo"), w("bo"), 1.0, None, ALU.mult)
                else:
                    t = dve.tensor_scalar(w("bo"), w("bo"), 0.3, None, ALU.mult)
                t.then_inc(L.prepared, 1)

            def ln_stats(m, p):
                dve.wait_ge(L.x_loaded, DMA * m + DMA)
                for b in range(BLK):
                    t = dve.bn_stats(B.stats[:, b, :], B.x[:, p, b * D:(b + 1) * D])
                t.then_inc(L.ln_stats, 1)
                (stats_count,) = worked_out(dve, 2 * m + 1)
                dve.wait_ge(consts_loaded, 2 * DMA)
                dve.wait_ge(L.ln_stats, stats_count)
                for b in range(BLK):
                    t = dve.bn_aggr(B.mv[:, b, :], B.stats[:, b, :])
                t.then_inc(L.ln_stats, 1)

            def ln_apply(m, p):
                dve.wait_ge(L.rstd_ready, m + 1)
                need(dve, L.xb_ready, m - 1)
                for b in range(BLK):
                    t = dve.tensor_scalar(B.xn[:, p, b * D:(b + 1) * D], B.x[:, p, b * D:(b + 1) * D],
                                          B.mv[:, b, 0:1], B.rstd[:, b:b + 1], ALU.subtract, ALU.mult)
                t.then_inc(L.xn_ready, 1)
                if l == 0:
                    dve.wait_ge(L.xn_ready, m + 1)
                    for b in range(BLK):
                        xb = B.xn[:, p, b * D:(b + 1) * D]
                        t = dve.tensor_tensor_reduce(B.sq[:, b * D:(b + 1) * D], xb, xb, 1.0, 0.0, ALU.mult, ALU.add,
                                                     B.ss[:, p, b:b + 1])
                    t.then_inc(L.sq_ready, 1)

            def rotate(m, q):
                tile, done = full(dve, L, m, "A", 1)
                for i, (b, table) in enumerate((("bq1", "cos"), ("bq2", "sin"), ("bk1", "cos"), ("bk2", "sin"))):
                    t = dve.scalar_tensor_tensor(B.rt[:, i, :], tile[:, i * S:(i + 1) * S], w(b), w(table),
                                                 ALU.add, ALU.mult)
                t.then_inc(done, 1)
                read(dve, L, m, "A", 1)
                rt = B.rt[:, :, :].rearrange("p (a r) t -> p a r t", r=2)
                dve.tensor_tensor(B.qk[:, :, :], rt[:, :, 0, :], rt[:, :, 1, :], ALU.add).then_inc(L.qk_ready, 1)

            def remainder(m, q):
                if L.rope:
                    src, ready = B.qk[:, :, :], L.res_ready
                else:
                    tile, ready = full(dve, L, m, "A", 1)
                    src = tile[:, 0:2 * S].rearrange("p (a t) -> p a t", a=2)
                dve.wait_ge(L.hi_ready, m + 1)
                need(dve, L.parts_ready, m)
                dve.tensor_tensor(B.res[:, :, :], src, B.parts[:, q, :, 0, :], ALU.subtract).then_inc(ready, 1)

            def values_in(m, q):
                tile, done = full(dve, L, m, "A", 2)
                need(dve, L.pv_done, L.TE * (m - 1))
                for j in range(4):
                    spread = B.V[:, q, :, :].rearrange("p b (i r) -> p b i r", r=P)[:, :, :, 40 * j:40 * j + HD]
                    v = tile[:, 0:BLK * D].rearrange("p (b i j d) -> p b i j d", b=BLK, i=4, j=4)[:, :, :, j, :]
                    bv = w("bv").rearrange("p (b i j d) -> p b i j d", b=BLK, i=4, j=4)[:, :, :, j, :]
                    t = dve.tensor_tensor(spread, v, bv, ALU.add)
                if l == 2:
                    t = dve.tensor_copy(B.gl[:, :, :], tile[:, BANK:BANK + 2 * E8].rearrange("p (b e) -> p b e", b=BLK))
                if l == 3:
                    t = dve.tensor_scalar(B.sel_h[:, :], tile[:, BANK:BANK + 1], w("bp1"), None, ALU.add)
                t.then_inc(done, 1)

            def token_qkv(m, q):
                tile, done = full(dve, L, m, "A", 3)
                dve.wait_ge(L.r_ready, m + 1)
                for b in range(BLK):
                    t = dve.scalar_tensor_tensor(B.tok[:, q, b, :], tile[:, b * BANK:b * BANK + 3 * D],
                                                 B.r1[:, q, b:b + 1], w("bqkv2"), ALU.mult, ALU.add)
                t.then_inc(done, 1)

            def route_in(m):
                read(dve, L, m, "A", 2)
                chain = Chain(dve, L.router, ROUTE, m)
                chain(dve.tensor_reduce(B.gs[:, :], B.gl[:, :, :], AX.X, ALU.max))
                dve.tensor_tensor(B.gl[:, :, :], B.gl[:, :, :], B.gs[:, :].unsqueeze(2).to_broadcast([P, BLK, E8]),
                                  ALU.subtract).then_inc(L.router_in, 1)

            def route(m, q):
                chain = Chain(dve, L.router, ROUTE, m)
                chain.i = 1
                dve.wait_ge(L.router_exp, m + 1)
                chain(dve.tensor_reduce(B.gs[:, :], B.gl[:, :, :], AX.X, ALU.add))
                chain(dve.reciprocal(B.gs[:, :], B.gs[:, :]))
                chain(dve.tensor_tensor(B.gl[:, :, :], B.gl[:, :, :],
                                        B.gs[:, :].unsqueeze(2).to_broadcast([P, BLK, E8]), ALU.mult), consts_loaded)
                dve.max(B.top[:, 0, :], B.gl[:, 0, :])
                chain(dve.max(B.top[:, 1, :], B.gl[:, 1, :]), consts_loaded)
                dve.max_index(B.idx[:, 0, :], B.top[:, 0, :], B.gl[:, 0, :])
                chain(dve.max_index(B.idx[:, 1, :], B.top[:, 1, :], B.gl[:, 1, :]))
                dve.tensor_copy(B.idxf[:, :, :], B.idx[:, :, 0:2])
                chain(dve.scalar_tensor_tensor(B.gs[:, :], B.top[:, :, 0], 1e-20, B.top[:, :, 1], ALU.add, ALU.add))
                chain(dve.reciprocal(B.gs[:, :], B.gs[:, :]))
                chain(dve.scalar_tensor_tensor(B.wt[:, :, :], B.top[:, :, 0:2], 2.5,
                                               B.gs[:, :].unsqueeze(2).to_broadcast([P, BLK, 2]), ALU.mult, ALU.mult))
                for b in range(BLK):
                    dve.tensor_scalar(B.one[:, b, :], c("iota"), B.idxf[:, b, 0:1], B.wt[:, b, 0:1], ALU.is_equal, ALU.mult)
                    t = dve.tensor_scalar(B.comb[:, q, b, :], c("iota"), B.idxf[:, b, 1:2], B.wt[:, b, 1:2],
                                          ALU.is_equal, ALU.mult)
                chain(t)
                chain(dve.tensor_tensor(B.comb[:, q, :, :], B.comb[:, q, :, :], B.one[:, :, :], ALU.add))

            def normalise(n):
                dve.wait_ge(L.pv_done, L.TE * n + L.TE)
                dve.reciprocal(B.rz[:, :], B.pOZ[:, S:2 * S]).then_inc(L.rz_ready, 1)
                dve.wait_ge(L.rz_ready, n + 1)
                need(dve, L.y_full, n)
                dve.tensor_tensor(B.on[:, :], B.pOZ[:, 0:S], B.rz[:, :], ALU.mult).then_inc(L.on_ready, 1)

            def maxima(m, *ks):
                for k in ks:
                    b, h0, heads, keys = m_tiles(L.causal)[k]
                    tile, done = full(dve, L, m, "M", k)
                    dve.tensor_reduce(B.nm[:, b, h0:h0 + heads], tile[:, :].rearrange("p (h k) -> p h k", k=keys),
                                      AX.X, ALU.max, negate=True).then_inc(done, 1)

            def split_max(m):
                for back in range(1, RING + 1):
                    read(dve, L, m, "M", L.TE - back)
                dve.tensor_copy(B.nms[:, :, 0, :], B.nm[:, :, :]).then_inc(L.max_split, 1)
                dve.wait_ge(L.max_split, 2 * m + 1)
                dve.tensor_tensor(B.nms[:, :, 1, :], B.nm[:, :, :], B.nms[:, :, 0, :], ALU.subtract).then_inc(L.max_split, 1)

            def token_scores(m, b):
                dve.wait_ge(L.prod_ready, 4 * m + b + 1)
                dve.tensor_reduce(B.att[:, b, :], B.prod[b].rearrange("p (a d) -> p a d", d=HD), AX.X, ALU.add)\
                   .then_inc(L.prod_read, 1)

            def token_views():
                att = B.att[:, :, :].rearrange("p b (h g) -> p (b h) g", g=H)
                am = B.am[:, :, :].rearrange("p b h -> p (b h)")
                return att, am, am.unsqueeze(2).to_broadcast([P, BLK * H, H])

            def token_softmax_in(m):
                att, am, spread = token_views()
                chain = Chain(dve, L.token, 3, m)
                dve.wait_ge(L.prod_read, 4 * m + 2)
                chain(dve.tensor_reduce(am, att, AX.X, ALU.max))
                dve.tensor_tensor(att, att, spread, ALU.subtract).then_inc(L.att_in, 1)

            def token_softmax_out(m):
                att, am, spread = token_views()
                chain = Chain(dve, L.token, 3, m)
                chain.i = 1
                dve.wait_ge(L.att_exp, m + 1)
                chain(dve.tensor_reduce(am, att, AX.X, ALU.add))
                chain(dve.reciprocal(am, am))
                dve.tensor_tensor(att, att, spread, ALU.mult).then_inc(L.att_ready, 1)

            def token_mix(n, p, b):
                dve.wait_ge(L.prod_ready, 4 * n + 3 + b)
                dve.tensor_reduce(B.mix[:, p, b * D:(b + 1) * D], B.prod[b].rearrange("p (a g) -> p a g", g=H),
                                  AX.X, ALU.add).then_inc(L.prod_read, 1)

            def sum_experts(n, b, first, weight, base):
                tile, done = full(dve, L, n, "F", first + b)
                for e in range(E8):
                    out, part = tile[:, e * D:(e + 1) * D], (base if e % 2 == 0 else B.acc[:, b, :])
                    if e > 1:
                        dve.wait_ge(L.experts_summed, 15 * n + (7 * b + e - 1))
                    if e == 1:
                        t = dve.tensor_scalar(part, out, weight(e), None, ALU.mult)
                    else:
                        t = dve.scalar_tensor_tensor(part, out, weight(e), part, ALU.mult, ALU.add)
                    t.then_inc(L.experts_summed if e < E8 - 1 else done, 1)

            def combine(n, first, base):
                for b in range(BLK):
                    read(dve, L, n, "F", first + b)
                acc = B.acc[:, :, :].rearrange("p b d -> p (b d)")
                dve.tensor_tensor(acc, acc, base, ALU.add).then_inc(L.experts_summed, 1)
                dve.wait_ge(L.experts_summed, 15 * n + 15)
                return acc

            def x1(n, p):
                tile, done = full(dve, L, n, "F", 1)
                dve.wait_ge(L.xb_ready, n + 1)
                dve.tensor_tensor(B.x1[:, :], tile[:, 0:S], B.x1b[:, p, :], ALU.add).then_inc(done, 1)
                read(dve, L, n, "F", 1)
                for b in range(BLK):
                    xb = B.x1[:, b * D:(b + 1) * D]
                    t = dve.tensor_tensor_reduce(B.sq[:, b * D:(b + 1) * D], xb, xb, 1.0, 0.0, ALU.mult, ALU.add,
                                                 B.ss2[:, b:b + 1])
                t.then_inc(L.sq2_ready, 1)

            def gate_in(n):
                tile, done = full(dve, L, n, "F", 3)
                dve.wait_ge(L.r2_ready, n + 1)
                chain = Chain(dve, L.router, 4, n)
                for b in range(BLK):
                    t = dve.scalar_tensor_tensor(B.gl[:, b, :], tile[:, b * E8:(b + 1) * E8], B.r2[:, b:b + 1],
                                                 w("bgate"), ALU.mult, ALU.add)
                t.then_inc(done, 1)
                read(dve, L, n, "F", 3)
                chain(dve.tensor_reduce(B.gs[:, :], B.gl[:, :, :], AX.X, ALU.max))
                dve.tensor_tensor(B.gl[:, :, :], B.gl[:, :, :], B.gs[:, :].unsqueeze(2).to_broadcast([P, BLK, E8]),
                                  ALU.subtract).then_inc(L.router_in, 1)

            def gate_out(n):
                chain = Chain(dve, L.router, 4, n)
                chain.i = 1
                dve.wait_ge(L.router_exp, n + 1)
                chain(dve.tensor_reduce(B.gs[:, :], B.gl[:, :, :], AX.X, ALU.add))
                chain(dve.reciprocal(B.gs[:, :], B.gs[:, :]))
                chain(dve.tensor_tensor(B.gs[:, :], B.gs[:, :], B.r2[:, :], ALU.mult))
                dve.tensor_tensor(B.gl[:, :, :], B.gl[:, :, :], B.gs[:, :].unsqueeze(2).to_broadcast([P, BLK, E8]),
                                  ALU.mult).then_inc(L.gate_ready, 1)
                dve.wait_ge(L.gate_ready, n + 1)

            def hidden(n, chunks, *ks):
                for k in ks:
                    tile, done = full(dve, L, n, "F", k)
                    width = S * min(2, chunks - 2 * k)
                    dve.wait_ge(L.gated, (chunks + 1) // 2 * n + (k + 1))
                    g = B.g[:, 2 * k:2 * k + width // S, :].rearrange("p a t -> p (a t)")
                    dve.tensor_tensor(g, tile[:, BANK:BANK + width], B.sg[:, k % 2, 0:width], ALU.mult).then_inc(done, 1)

            def choice_views():
                sel = B.sel
                return sel[0:1, 0:E8], sel[0:1, E8:2 * E8], sel[0:1, 2 * E8:2 * E8 + 1], sel[0:1, 3 * E8:3 * E8 + 1]

            def choose_in(m):
                lg, top, small, total = choice_views()
                chain = Chain(dve, L.choice, 5, m)
                tile, done = full(dve, L, m, "R", 0)
                dve.tensor_tensor(lg, tile[0:1, 0:E8], w("bp2")[0:1, :], ALU.add).then_inc(done, 1)
                read(dve, L, m, "R", 0)
                chain(dve.tensor_reduce(small, lg, AX.X, ALU.max, negate=True))
                dve.tensor_scalar(total, small, 1.0, None, ALU.mult).then_inc(L.choice_in, 1)

            def choose_out(m):
                lg, top, small, total = choice_views()
                chain = Chain(dve, L.choice, 5, m)
                chain.i = 1
                dve.wait_ge(L.choice_exp, m + 1)
                chain(dve.tensor_reduce(total, lg, AX.X, ALU.add))
                chain(dve.reciprocal(total, total))
                chain(dve.tensor_scalar(lg, lg, total, None, ALU.mult), consts_loaded)
                chain(dve.max(top, lg), consts_loaded)
                need(dve, L.chosen, m)
                dve.max_index(B.sel_i[0:1, :], top, lg).then_inc(L.choice_ready, 1)

            def expert_output(n, p):
                tile, done = full(dve, L, n, "F", 1)
                dve.wait_ge(L.chosen, n + 1)
                dve.tensor_scalar(B.rT[:, :], tile[:, 0:S], B.wsel[:, p, 514:515], 0.3, ALU.add, ALU.mult).then_inc(done, 1)

            def finish(n, p, base):
                dve.wait_ge(L.y_full, n + 1)
                need(dve, L.x_stored, DMA * (n - 1))
                dve.tensor_tensor(B.xo[:, p, :], B.pY[:, 0:S], base, ALU.add).then_inc(L.residual_done, 1)

            def expert_sum(b):
                def action(m, p):
                    dve.wait_ge(L.xb_ready, m + 1)
                    sum_experts(m, b, 8, lambda e: B.comb[:, p, b, e:e + 1], B.xb[:, p, b * D:(b + 1) * D])
                return action

            def last_sum(m, p):
                if l == 0:
                    dve.wait_ge(L.xx_ready, m + 1)
                    base = B.xx[:, :]
                elif l == 2:
                    base = combine(m, 8, B.xb[:, p, :])
                else:
                    dve.wait_ge(L.xb_ready, m + 1)
                    base = B.xb[:, p, :]
                finish(m, p, base)

            actions = {
                "stats": (3, ln_stats), "norm": (3, ln_apply), "A1": (2, rotate), "rest": (2, remainder), "A2": (2, values_in),
                "A3": (2, token_qkv), "split": (1, lambda m, p: split_max(m)), "V": (0, lambda m, p: normalise(m)),
                "finish": (0, last_sum)}
            for k in range(L.TE):
                actions[f"M{k}"] = (1, lambda m, p, k=k: maxima(m, k))
            if l == 0:
                actions.update({
                    "scores0": (1, lambda m, p: token_scores(m, 0)), "scores1": (1, lambda m, p: token_scores(m, 1)),
                    "softmax_in": (1, lambda m, p: token_softmax_in(m)), "softmax_out": (1, lambda m, p: token_softmax_out(m)),
                    "mix0": (1, lambda m, p: token_mix(m, p, 0)), "mix1": (0, lambda m, p: token_mix(m, p, 1)),
                    "F1": (0, x1), "F3": (0, lambda m, p: gate_in(m)), "gate": (0, lambda m, p: gate_out(m))})
            if l in (1, 2):
                for k in range(8):
                    actions[f"F{k}"] = (0, lambda m, p, k=k: hidden(m, (0, HID1, CH2)[l], k))
            if l == 2:
                actions.update({"route_in": (1, lambda m, p: route_in(m)), "route": (1, route),
                                "F8": (0, expert_sum(0)), "F9": (0, expert_sum(1))})
            if l == 3:
                actions.update({"R0": (1, lambda m, p: choose_in(m)), "chosen": (1, lambda m, p: choose_out(m)),
                                "F1": (0, expert_output)})
            prepare()
            steps(dve, in_order(VECTOR_ORDER[l], actions))


def gpsimd_program(nc, block, B, layer_state, read, c, consts_loaded, cleared, w_loaded):
    @block.gpsimd
    def _(pool):
        pool.memset(B.V[:, :, :, :], 0.0).then_inc(cleared, 1)
        for i in range(2):
            pool.wait_ge(cleared, 2 * i + 1)
            pool.memset(B.KS[i][64:128, :, :], 1.0).then_inc(cleared, 1)
            pool.wait_ge(cleared, 2 * i + 2)
            pool.memset(B.QS[i][64:128, :, :], 0.0).then_inc(cleared, 1)
        pool.wait_ge(cleared, 5)
        pool.wait_ge(consts_loaded, 2 * DMA)
        for L in layer_state:
            l, w = L.l, L.w
            power = c("neghalf")[:, 0:BLK]

            def rstd(m):
                stats_count, rstd_count = worked_out(pool, 2 * m + 2, m)
                pool.wait_ge(consts_loaded, 2 * DMA)
                pool.wait_ge(L.ln_stats, stats_count)
                need(pool, L.rstd_ready, rstd_count)
                pool.tensor_scalar(B.ve[:, :], B.mv[:, :, 1], 1e-5, None, ALU.add).then_inc(L.ln_var, 1)
                pool.wait_ge(L.ln_var, m + 1)
                need(pool, L.xn_ready, m)
                pool.tensor_tensor(B.rstd[:, :], B.ve[:, :], power, ALU.pow).then_inc(L.rstd_ready, 1)

            def inverse_rms(m, sums, mean, out, ready_in, between, ready_out):
                in_count, out_count = worked_out(pool, m + 1, m)
                pool.wait_ge(consts_loaded, 2 * DMA)
                pool.wait_ge(ready_in, in_count)
                need(pool, ready_out, out_count)
                pool.tensor_scalar(mean, sums, 1.0 / D, 1e-6, ALU.mult, ALU.add).then_inc(between, 1)
                pool.wait_ge(between, m + 1)
                pool.tensor_tensor(out, mean, power, ALU.pow).then_inc(ready_out, 1)

            def base(m, p):
                pool.wait_ge(L.xn_ready, m + 1)
                need(pool, L.residual_done, m - 1)
                t = pool.tensor_tensor(B.xb[:, p, :], B.x[:, p, :], w("bo"), ALU.add)
                if l == 0:
                    t = pool.tensor_tensor(B.x1b[:, p, :], B.xn[:, p, :], w("bo2"), ALU.add)
                if l == 3:
                    t.then_inc(L.pool_sum, 1)
                    pool.wait_ge(L.pool_sum, m + 1)
                    t = pool.tensor_tensor(B.xb[:, p, :], B.xb[:, p, :], B.xn[:, p, :], ALU.add)
                t.then_inc(L.xb_ready, 1)

            def lowest(m, q):
                pool.wait_ge(L.mid_ready, m + 1)
                pool.tensor_tensor(B.parts[:, q, :, 2, :], B.res[:, :, :], B.parts[:, q, :, 1, :], ALU.subtract)\
                    .then_inc(L.parts_ready, 1)

            def score_products(m, q, *bs):
                read(pool, L, m, "A", 3)
                for b in bs:
                    need(pool, L.prod_read, 4 * m + (b - 1))
                    qh = B.tok[:, q, b, 0:D].rearrange("p (h d) -> p h d", d=HD).unsqueeze(2).to_broadcast([P, H, H, HD])
                    kg = B.tok[:, q, b, D:2 * D].rearrange("p (g d) -> p g d", d=HD).unsqueeze(1).to_broadcast([P, H, H, HD])
                    pool.tensor_tensor(B.prod[b].rearrange("p (h g d) -> p h g d", h=H, g=H), qh, kg, ALU.mult)\
                        .then_inc(L.prod_ready, 1)

            def value_products(m, q):
                pool.wait_ge(L.att_ready, m + 1)
                for b in range(BLK):
                    ah = B.att[:, b, :].rearrange("p (h g) -> p h g", h=H).unsqueeze(2).to_broadcast([P, H, HD, H])
                    vd = B.tok[:, q, b, 2 * D:3 * D].rearrange("p (d g) -> p d g", d=HD).unsqueeze(1)\
                        .to_broadcast([P, H, HD, H])
                    pool.tensor_tensor(B.prod[b].rearrange("p (h d g) -> p h d g", h=H, d=HD), ah, vd, ALU.mult)\
                        .then_inc(L.prod_ready, 1)

            def second_norm(n, p):
                inverse_rms(n, B.ss2[:, :], B.sv[:, 0, :], B.r2[:, :], L.sq2_ready, L.sv2_ready, L.r2_ready)
                read(pool, L, n, "F", 1)
                pool.tensor_tensor(B.xx[:, :], B.x1[:, :], B.xb[:, p, :], ALU.add).then_inc(L.xx_ready, 1)

            def choose(m, q):
                (choice_count,) = worked_out(pool, m + 1)
                pool.wait_ge(consts_loaded, 2 * DMA)
                pool.wait_ge(L.choice_ready, choice_count)
                e = pool.value_load(B.sel_i[0:1, 0:1], min_val=0, max_val=E8 - 1)
                need(pool, L.y_full, m - 1)
                pool.tensor_copy(B.wsel[:, q, :], w("experts")[:, bass.ds(e * EXP3, EXP3)]).then_inc(L.chosen, 1)

            actions = {
                "rstd": (3, lambda m, p: rstd(m)), "lowest": (2, lowest), "base": (2, base),
                "inverse_rms": (3, lambda m, p: inverse_rms(m, B.ss[:, p, :], B.sv[:, 1, :], B.r1[:, p, :],
                                                            L.sq_ready, L.sv_ready, L.r_ready)),
                "products0": (2, lambda m, p: score_products(m, p, 0)), "products1": (1, lambda m, p: score_products(m, p, 1)),
                "x1": (0, second_norm), "values": (1, value_products), "choose": (1, choose)}
            pool.wait_ge(L.prepared, 2 if l == 0 else 1)
            steps(pool, in_order(GPSIMD_ORDER[l], actions))


ROUTE = 11


def rope_tables():
    t = np.arange(S, dtype=np.float32)
    inv8 = (np.float32(1.0) / np.float32(10000.0) ** (np.arange(0, HD, 2, dtype=np.float32) / np.float32(HD)))
    f8 = t[:, None] * inv8[None, :].astype(np.float32)
    mixed = np.concatenate([np.sin(f8), np.cos(f8)], axis=-1)
    inv2 = (np.float32(1.0) / np.float32(500.0) ** (np.arange(4, dtype=np.float32) / np.float32(4)))
    f2 = t[:, None] * inv2[None, :].astype(np.float32)
    out = {1: (mixed[:, 1::2], mixed[:, 0::2]), 2: (np.cos(f2), np.sin(f2)), 3: (np.cos(f8), np.sin(f8))}
    rows = {}
    for l, (cos, sin) in out.items():
        cos8 = np.concatenate([cos, cos], axis=1).T
        sin8 = np.concatenate([-sin, sin], axis=1).T
        rows[l] = (np.repeat(cos8, H, axis=0).astype(np.float32), np.repeat(sin8, H, axis=0).astype(np.float32))
    return rows


ROTATE = {1: ([0, 2, 4, 6, 1, 3, 5, 7], [1, 3, 5, 7, 0, 2, 4, 6]), 2: (list(range(8)), [4, 5, 6, 7, 0, 1, 2, 3]),
          3: (list(range(8)), [4, 5, 6, 7, 0, 1, 2, 3])}


def constants():
    const = np.zeros((P, CONST_N), np.float32)
    const[:, :P] = np.eye(P)
    a = CONST["ones"][0]
    for j in range(4):
        const[:, a + 32 * j + HD * j:a + 32 * j + HD * j + HD] = 1.0
    const[:, CONST["iota"][0]:CONST["iota"][1]] = np.arange(E8)
    const[:, CONST["neghalf"][0]:CONST["neghalf"][1]] = -0.5
    above = np.where(np.arange(P)[None, :] > np.arange(P)[:, None], MASKED, 0.0)
    constb = np.concatenate([np.eye(P), above, above, above.T, above.T], axis=1).astype(np.float32)
    return const, constb


def layouts(a):
    f = lambda x: np.asarray(x)
    table = rope_tables()

    def rows(x):
        return np.broadcast_to(f(x)[None, :], (P, f(x).shape[0]))

    def by_dim(wm, dims):
        return np.stack([wm.reshape(wm.shape[0], H, HD)[:, :, d] for d in dims], axis=1).reshape(wm.shape[0], H * HD)

    def padded(wm, n):
        out = np.zeros((n,) + wm.shape[1:], wm.dtype)
        out[:wm.shape[0]] = wm
        return out

    def column(v):
        return f(v).reshape(P, 1)

    packs = []
    def heads8(wm):
        out = np.zeros((P, H, HD), np.float32)
        out[:wm.shape[0], :, :4] = wm.reshape(wm.shape[0], H, 4)
        return out.reshape(P, H * HD)
    Wq, Wk, Wv = (heads8(f(a["L0_attn_" + n]).T) for n in ("Wq", "Wk", "Wv"))
    Wo = np.zeros((H, HD, D), np.float32)
    Wo[:, :4] = f(a["L0_attn_Wo"]).T.reshape(H, 4, D)
    up = f(a["L0_ffn_Wup"]).reshape(64, H, 2, HD)
    bup = f(a["L0_ffn_bup"]).reshape(H, 2, HD)
    kv = lambda x: np.concatenate([x[..., :, 0, :].reshape(x.shape[:-3] + (D,)),
                                   np.swapaxes(x[..., :, 1, :], -1, -2).reshape(x.shape[:-3] + (D,))], axis=-1)
    bdown = np.zeros((P, P), np.float32)
    bdown[:64] = f(a["L0_ffn_bdown"])[:, None]
    zeros = lambda n: np.zeros((P, n), np.float32)
    packs.append(dict(
        q1=by_dim(Wq, range(HD)), k1=by_dim(Wk, range(HD)), v=Wv, bv=zeros(BLK * D), o=Wo.reshape(P, D),
        bo=np.tile(rows(a["L0_attn_bo"]), (1, BLK)), qkv2=np.concatenate([f(a["L0_ffn_Wq"]), zeros(2 * D)], axis=1),
        down=padded(f(a["L0_ffn_Wdown"]).T, P), up=padded(kv(up), P), bdown=bdown, bup=rows(kv(bup)),
        bqkv2=np.concatenate([rows(a["L0_ffn_bq"]), zeros(2 * D)], axis=1), g1=column(a["L0_ffn_gamma1"]),
        g2=column(a["L0_ffn_gamma2"]), o2=f(a["L0_ffn_Wo"]), bo2=np.tile(rows(a["L0_ffn_bo"]), (1, BLK)),
        gate=f(a["L0_ffn_Wg"]), bgate=rows(a["L0_ffn_bg"]),
        experts=f(a["L0_ffn_We"]).transpose(1, 0, 2).reshape(D, E8 * D)))

    def attention(l, wq, wk, wv, bq, bk, bv, wo, bo):
        d1, d2 = ROTATE[l]
        cos, sin = table[l]
        return dict(q1=by_dim(wq, d1), q2=by_dim(wq, d2), k1=by_dim(wk, d1), k2=by_dim(wk, d2), cos=cos, sin=sin,
                    bq1=by_dim(bq[None], d1).reshape(P, 1), bq2=by_dim(bq[None], d2).reshape(P, 1),
                    bk1=by_dim(bk[None], d1).reshape(P, 1), bk2=by_dim(bk[None], d2).reshape(P, 1),
                    v=wv, bv=np.tile(rows(bv), (1, BLK)), o=wo, bo=np.tile(rows(bo), (1, BLK)))

    w, b = f(a["L1_attn_qkv_w"]), f(a["L1_attn_qkv_b"])
    packs.append(attention(1, w[:, :D], w[:, D:2 * D], w[:, 2 * D:], b[:D], b[D:2 * D], b[2 * D:],
                           f(a["L1_attn_out_w"]), a["L1_attn_out_b"]))
    ints = np.concatenate([f(a["L1_ffn_w_gate"]).T, f(a["L1_ffn_w_up"]).T] +
                          [f(a["L1_ffn_w_down"]).T[i * P:(i + 1) * P] for i in range(HID1)], axis=1)

    w, b = f(a["L2_attn_w_qkv"]), f(a["L2_attn_b_qkv"])
    pack = attention(2, w[:, :D], w[:, D:2 * D], w[:, 2 * D:], b[:D], b[D:2 * D], b[2 * D:],
                     f(a["L2_attn_w_out"]), a["L2_attn_b_out"])

    def chunks(experts, shared):
        out = np.zeros((P, CH2, P), np.float32)
        for e in range(E8):
            out[:, e] = experts[e][:, :P]
            out[:, E8 + e // 2, 64 * (e % 2):64 * (e % 2) + 48] = experts[e][:, P:]
        for s in range(3):
            part = shared[:, s * P:(s + 1) * P]
            out[:, 12 + s, :part.shape[1]] = part
        return out.reshape(P, CH2 * P)
    down, shared = f(a["L2_ffn_w_down"]), f(a["L2_ffn_sw_down"])
    rest = np.zeros((P, E8, D), np.float32)
    for e in range(E8):
        rest[64 * (e % 2):64 * (e % 2) + 48, e] = down[e][P:]
    pack.update(
        router=f(a["L2_ffn_gate_w"]).T, gate=chunks(f(a["L2_ffn_w_gate"]), f(a["L2_ffn_sw_gate"])),
        up=chunks(f(a["L2_ffn_w_up"]), f(a["L2_ffn_sw_up"])), down=down[:, :P].transpose(1, 0, 2).reshape(P, E8 * D),
        downr=rest.reshape(P, E8 * D), shared=padded(shared, 3 * P).reshape(3, P, D).transpose(1, 0, 2).reshape(P, 3 * D))
    packs.append(pack)

    nothing = np.zeros(D, np.float32)
    pack = attention(3, f(a["L3_attn_Wq"]).T, f(a["L3_attn_Wk"]).T, f(a["L3_attn_Wv"]).T, nothing, nothing, nothing,
                     f(a["L3_attn_Wo"]).T, a["L3_ffn_bo"])
    w1, b1, w2, b2 = (f(a["L3_ffn_" + n]) for n in ("W1", "b1", "W2", "b2"))
    pack.update(
        p1=f(a["L3_ffn_Wp1"]), bp1=column(a["L3_ffn_bp1"]), p2=f(a["L3_ffn_Wp2"]), bp2=rows(a["L3_ffn_bp2"]),
        experts=np.concatenate([np.concatenate([w1[e], w2[e][:P], w2[e][P:], b1[e].reshape(2, P).T, b2[e].reshape(P, 1)],
                                               axis=1) for e in range(E8)], axis=1), o3=f(a["L3_ffn_Wo"]))
    packs.append(pack)
    laid = []
    for (fields, n), pack in zip(WEIGHTS, packs):
        out = np.zeros((P, n), np.float32)
        for name, (i, j) in fields.items():
            if name != "ffn":
                out[:, i:j] = pack[name]
        laid.append(out)
    return laid, np.ascontiguousarray(ints)


def program(nc, arrays, layers=LAYERS):
    aps = {}
    for name, v in arrays.items():
        aps[name.removesuffix("_dram")] = nc.dram_tensor(name, v.shape, mybir.dt.from_np(v.dtype), kind="ExternalInput").ap()
    out = nc.dram_tensor("out_dram", (NB * S, D), F32, kind="ExternalOutput").ap()
    build(nc, aps["x"], [aps[f"w{l}"] for l in range(4)], aps["ints"], aps["const"], aps["constb"], out, layers)


def arrange(inputs):
    laid, ints = layouts(inputs)
    const, constb = constants()
    arrays = {"x": np.ascontiguousarray(np.asarray(inputs["L0_attn_x"]).reshape(NB * S, D)), "ints": ints,
              "const": const, "constb": constb}
    for l, w in enumerate(laid):
        arrays[f"w{l}"] = w
    return {f"{name}_dram": v for name, v in arrays.items()}


def kernel(**inputs):
    import concourse.bacc as bacc
    from concourse.bass_utils import run_bass_kernel_spmd
    arrays = arrange(inputs)
    nc = bacc.Bacc("TRN2", target_bir_lowering=False, num_devices=1)
    program(nc, arrays)
    r = run_bass_kernel_spmd(nc, [arrays], core_ids=[0])
    return r.results[0]["out_dram"].reshape(NB, S, D)
```
